# Optimizing a Trainium2 kernel written in Bass

```python
import numpy as np
import jax
import jax.numpy as jnp

def _softmax(x, axis=-1):
    return jax.nn.softmax(x, axis=axis)

def _gelu(x):
    return jax.nn.gelu(x, approximate=True)

def _silu(x):
    return jax.nn.silu(x)

def _sigmoid(x):
    return jax.nn.sigmoid(x)

def _layernorm(x, axis=-1, eps=1e-05):
    m = jnp.mean(x, axis=axis, keepdims=True)
    v = jnp.var(x, axis=axis, keepdims=True)
    return (x - m) / jnp.sqrt(v + eps)

def _scatter_add(tgt, idx, src, axis=0):
    return tgt.at[idx].add(src)

def _segment_sum(src, seg, n):
    return jax.ops.segment_sum(src, seg, n)
kernel_name = 'mk_decoder_preln_d1_seqx_r4_112c0a'

def setup_inputs(seed: int=0):
    np.random.seed(seed)
    _w = jnp.asarray

    def _rec_inputs():
        import jax
        import jax.numpy as jnp
        _rk = jax.random.key(seed)
        x = -0.0003929 + 0.9999 * jax.random.normal(jax.random.fold_in(_rk, 1), (32, 256, 256), jnp.float32)
        _lenS = 256 - jax.random.randint(jax.random.fold_in(_rk, 7), (32,), 0, max(1, 256 // 4) + 1, jnp.int32)
        _lenS2 = 256 - jax.random.randint(jax.random.fold_in(_rk, 8), (32,), 0, max(1, 256 // 4) + 1, jnp.int32)
        _ctx_1024P = jax.random.normal(jax.random.fold_in(_rk, 11), (32, 16, 256), jnp.float32)
        _ctx_1024c = jax.random.dirichlet(jax.random.fold_in(_rk, 511), 0.3 * jnp.ones((16,), jnp.float32), (32, 256))
        _ctx_1024t = jnp.einsum('bsk,bkd->bsd', _ctx_1024c, _ctx_1024P)
        _ctx_1024t = _ctx_1024t * jax.lax.rsqrt(jnp.mean(jnp.square(_ctx_1024t)) + 1e-12) * 0.953939
        ctx_1024 = 0.00208318 + 0.999174 * (_ctx_1024t + 0.3 * jax.random.normal(jax.random.fold_in(_rk, 611), (32, 256, 256), jnp.float32))
        _validS = jnp.arange(256)[None, :] < _lenS[:, None]
        _validS2 = jnp.arange(256)[None, :] < _lenS2[:, None]
        _causal = jnp.tril(jnp.ones((256, 256), dtype=bool))
        mask_BxSxS2_ff0 = jnp.where(jnp.ones((32, 256, 256), dtype=bool), 0.0, -1000000000.0).astype(jnp.float32)
        return (x, ctx_1024, mask_BxSxS2_ff0)
    x, ctx_1024, mask_BxSxS2_ff0 = _rec_inputs()

    def _L0_attn_setup():
        import jax, jax.numpy as jnp
        import numpy as np
        HEADS = 16
        EPS = 1e-06
        key = jax.random.key(seed)
        k1, k2, k3 = jax.random.split(key, 3)
        B, N, C = (4, 1024, 256)
        x = jax.random.normal(k1, (B, N, C), dtype=jnp.float32)
        w_qkv = jax.random.normal(k2, (3 * C, C), dtype=jnp.float32) * C ** (-0.5)
        w_out = jax.random.normal(k3, (C, C), dtype=jnp.float32) * C ** (-0.5)
        b_out = jnp.zeros((C,), dtype=jnp.float32)
        return {'x': x, 'w_qkv': w_qkv, 'w_out': w_out, 'b_out': b_out}
    _L0_attn_all = _L0_attn_setup()
    _L0_attn_in = {k: v for k, v in _L0_attn_all.items() if k in ('w_qkv', 'w_out', 'b_out')}
    del _L0_attn_all

    def _L0_xattn_setup():
        import jax, jax.numpy as jnp
        import numpy as np
        NUM_HEADS = 16
        DIM = 256
        key = jax.random.key(seed)
        ks = jax.random.split(key, 12)
        B, N, T, C = (4, 1024, 77, DIM)
        s = 1.0 / np.sqrt(C)
        return {'hidden_states': jax.random.normal(ks[0], (B, N, C), jnp.float32), 'encoder_hidden_states': jax.random.normal(ks[1], (B, T, C), jnp.float32), 'attention_mask': jnp.zeros((B, N, T), jnp.float32), 'Wq': jax.random.normal(ks[2], (C, C), jnp.float32) * s, 'bq': jnp.zeros((C,), jnp.float32), 'Wk': jax.random.normal(ks[3], (C, C), jnp.float32) * s, 'bk': jnp.zeros((C,), jnp.float32), 'Wv': jax.random.normal(ks[4], (C, C), jnp.float32) * s, 'bv': jnp.zeros((C,), jnp.float32), 'Wo': jax.random.normal(ks[5], (C, C), jnp.float32) * s, 'bo': jnp.zeros((C,), jnp.float32)}
    _L0_xattn_all = _L0_xattn_setup()
    _L0_xattn_in = {k: v for k, v in _L0_xattn_all.items() if k in ('Wq', 'bq', 'Wk', 'bk', 'Wv', 'bv', 'Wo', 'bo')}
    del _L0_xattn_all

    def _L0_ffn_setup():
        import jax, jax.numpy as jnp
        import numpy as np
        key = jax.random.key(seed)
        ks = jax.random.split(key, 6)
        B, L, D, E = (4, 512, 256, 4)
        H = 4 * D
        x = jax.random.normal(ks[0], (B, L, D), dtype=jnp.float32)
        rW1 = jax.random.normal(ks[1], (D, 2 * D), dtype=jnp.float32) * (2.0 / D) ** 0.5
        rb1 = jnp.zeros((2 * D,), dtype=jnp.float32)
        rW2 = jax.random.normal(ks[2], (2 * D, E), dtype=jnp.float32) * (2.0 / (2 * D)) ** 0.5
        rb2 = jnp.zeros((E,), dtype=jnp.float32)
        We1 = jax.random.normal(ks[3], (E, D, H), dtype=jnp.float32) * (2.0 / D) ** 0.5
        be1 = jnp.zeros((E, H), dtype=jnp.float32)
        We2 = jax.random.normal(ks[4], (E, H, D), dtype=jnp.float32) * (2.0 / H) ** 0.5
        be2 = jnp.zeros((E, D), dtype=jnp.float32)
        return {'x': x, 'rW1': rW1, 'rb1': rb1, 'rW2': rW2, 'rb2': rb2, 'We1': We1, 'be1': be1, 'We2': We2, 'be2': be2}
    _L0_ffn_all = _L0_ffn_setup()
    _L0_ffn_in = {k: v for k, v in _L0_ffn_all.items() if k in ('rW1', 'rb1', 'rW2', 'rb2', 'We1', 'be1', 'We2', 'be2')}
    del _L0_ffn_all
    return {'x': x, 'ctx_1024': ctx_1024, 'mask_BxSxS2_ff0': mask_BxSxS2_ff0, 'L0_attn_w_qkv': _L0_attn_in['w_qkv'], 'L0_attn_w_out': _L0_attn_in['w_out'], 'L0_attn_b_out': _L0_attn_in['b_out'], 'L0_xattn_Wq': _L0_xattn_in['Wq'], 'L0_xattn_bq': _L0_xattn_in['bq'], 'L0_xattn_Wk': _L0_xattn_in['Wk'], 'L0_xattn_bk': _L0_xattn_in['bk'], 'L0_xattn_Wv': _L0_xattn_in['Wv'], 'L0_xattn_bv': _L0_xattn_in['bv'], 'L0_xattn_Wo': _L0_xattn_in['Wo'], 'L0_xattn_bo': _L0_xattn_in['bo'], 'L0_ffn_rW1': _L0_ffn_in['rW1'], 'L0_ffn_rb1': _L0_ffn_in['rb1'], 'L0_ffn_rW2': _L0_ffn_in['rW2'], 'L0_ffn_rb2': _L0_ffn_in['rb2'], 'L0_ffn_We1': _L0_ffn_in['We1'], 'L0_ffn_be1': _L0_ffn_in['be1'], 'L0_ffn_We2': _L0_ffn_in['We2'], 'L0_ffn_be2': _L0_ffn_in['be2']}

def reference(x, ctx_1024, mask_BxSxS2_ff0, L0_attn_w_qkv, L0_attn_w_out, L0_attn_b_out, L0_xattn_Wq, L0_xattn_bq, L0_xattn_Wk, L0_xattn_bk, L0_xattn_Wv, L0_xattn_bv, L0_xattn_Wo, L0_xattn_bo, L0_ffn_rW1, L0_ffn_rb1, L0_ffn_rW2, L0_ffn_rb2, L0_ffn_We1, L0_ffn_be1, L0_ffn_We2, L0_ffn_be2):
    import jax
    import jax.numpy as jnp

    def _L0_attn_ref(x, w_qkv, w_out, b_out):
        import jax, jax.numpy as jnp
        import numpy as np
        HEADS = 16
        EPS = 1e-06
        B, N, C = x.shape
        H = HEADS
        D = C // H
        scale = D ** (-0.25)
        qkv = x @ w_qkv.T
        q, k, v = jnp.split(qkv, 3, axis=-1)

        def heads(t):
            return t.reshape(B, N, H, D).transpose(0, 2, 1, 3)
        q, k, v = (heads(q), heads(k), heads(v))
        feat = lambda t: jax.nn.elu(t) + 1.0
        q = feat(q) * scale
        k = feat(k) * scale
        kv = jnp.einsum('bhnd,bhne->bhde', k, v)
        out = jnp.einsum('bhnd,bhde->bhne', q, kv)
        k_sum = k.sum(axis=2)
        denom = jnp.einsum('bhnd,bhd->bhn', q, k_sum)
        out = out / (denom[..., None] + EPS)
        out = out.transpose(0, 2, 1, 3).reshape(B, N, C)
        return out @ w_out.T + b_out

    def _L0_xattn_ref(hidden_states, encoder_hidden_states, attention_mask, Wq, bq, Wk, bk, Wv, bv, Wo, bo):
        import jax, jax.numpy as jnp
        import numpy as np
        NUM_HEADS = 16
        DIM = 256
        B, N, C = hidden_states.shape
        T = encoder_hidden_states.shape[1]
        H = NUM_HEADS
        D = C // H
        q = (hidden_states @ Wq.T + bq).reshape(B, N, H, D).transpose(0, 2, 1, 3)
        k = (encoder_hidden_states @ Wk.T + bk).reshape(B, T, H, D).transpose(0, 2, 1, 3)
        v = (encoder_hidden_states @ Wv.T + bv).reshape(B, T, H, D).transpose(0, 2, 1, 3)
        scale = 1.0 / jnp.sqrt(jnp.asarray(D, q.dtype))
        scores = jnp.einsum('bhnd,bhtd->bhnt', q, k) * scale + attention_mask[:, None, :, :]
        attn = jax.nn.softmax(scores, axis=-1)
        out = jnp.einsum('bhnt,bhtd->bhnd', attn, v)
        out = out.transpose(0, 2, 1, 3).reshape(B, N, C)
        return out @ Wo.T + bo

    def _L0_ffn_ref(x, rW1, rb1, rW2, rb2, We1, be1, We2, be2):
        import jax, jax.numpy as jnp
        import numpy as np
        E = We1.shape[0]
        top_k = min(2, E)
        rh = jax.nn.gelu(x @ rW1 + rb1, approximate=False)
        router_logits = rh @ rW2 + rb2
        router_probs = jax.nn.softmax(router_logits, axis=-1)
        expert_weights, expert_indices = jax.lax.top_k(router_probs, top_k)
        one_hot = jax.nn.one_hot(expert_indices, E, dtype=x.dtype)
        token_mask = one_hot.sum(axis=2)
        combine_w = (one_hot * expert_weights[..., None]).sum(axis=2)
        out = jnp.zeros_like(x)
        for e in range(E):
            xi = x * token_mask[..., e:e + 1]
            h = jax.nn.gelu(xi @ We1[e] + be1[e], approximate=False)
            yo = h @ We2[e] + be2[e]
            out = out + yo * combine_w[..., e:e + 1]
        return out
    x = x + _L0_attn_ref(_layernorm(x, axis=-1), L0_attn_w_qkv, L0_attn_w_out, L0_attn_b_out)
    x = x + _L0_xattn_ref(_layernorm(x, axis=-1), ctx_1024, mask_BxSxS2_ff0, L0_xattn_Wq, L0_xattn_bq, L0_xattn_Wk, L0_xattn_bk, L0_xattn_Wv, L0_xattn_bv, L0_xattn_Wo, L0_xattn_bo)
    x = x + _L0_ffn_ref(_layernorm(x, axis=-1), L0_ffn_rW1, L0_ffn_rb1, L0_ffn_rW2, L0_ffn_rb2, L0_ffn_We1, L0_ffn_be1, L0_ffn_We2, L0_ffn_be2)
    return x

_drawn_inputs = setup_inputs


def setup_inputs(seed=0):
    import zlib

    import numpy as np

    out = dict(_drawn_inputs(seed))
    spreads = {'L0_attn_b_out': (0.0, 0.1),
     'L0_xattn_bq': (0.0, 0.1),
     'L0_xattn_bk': (0.0, 0.1),
     'L0_xattn_bv': (0.0, 0.1),
     'L0_xattn_bo': (0.0, 0.1),
     'L0_ffn_rb1': (0.0, 0.1),
     'L0_ffn_rb2': (0.0, 0.1),
     'L0_ffn_be1': (0.0, 0.1),
     'L0_ffn_be2': (0.0, 0.1)}
    factors = {}
    for name, (base, spread) in spreads.items():
        noise = np.random.default_rng([zlib.crc32(name.encode()), seed]).standard_normal(out[name].shape)
        drawn = base * np.exp(spread * noise) if base else spread * noise
        out[name] = jnp.asarray(drawn.astype(out[name].dtype))
    for name, factor in factors.items():
        out[name] = (out[name] * factor).astype(out[name].dtype)
    return out
```

```python
from contextlib import ExitStack

import concourse.bass as bass
from concourse import mybir

P = 128
F32 = mybir.dt.float32
F32R = mybir.dt.float32r
ALU = mybir.AluOpType
ACT = mybir.ActivationFunctionType
AX = mybir.AxisListType
LN_EPS = 1e-5


def wait(engine, semaphore, value):
    if not isinstance(value, int) or value > 0:
        engine.wait_ge(semaphore, value)
DEN_EPS = 1e-6
HEADS = 16
BIG = 3.0e38


def wait_apart(engine, semaphore, value, passed):
    wait(engine, semaphore, value)
    engine.sem_inc(passed, 1)


def build_attention(nc, x, ctx_in, mask, ident_in, block_in, heads_in, wqkvT, woutT, b_out, wqT, bq, wkT, bk, wvT, bv,
                    woT, bo, qk_dram, x2):
    B, S, C = x.shape
    H = HEADS
    D = C // H
    T = S // P
    KC = C // P
    SCALE = D ** -0.5
    HB = P // D
    HP = H // 2
    G = H // 4
    W1 = P + HB
    with ExitStack() as ctx:
        def sb(name, shape, dt=F32):
            return ctx.enter_context(nc.sbuf_tensor("a_" + name, shape, dt))

        def sem(name):
            return ctx.enter_context(nc.semaphore("a_" + name))

        def pair(name, shape):
            return sb(name + "h", shape, F32R), sb(name + "l", shape, F32R)

        NW = 8
        LQ, LK, LV, LO, CQ, CK, CV, CO = range(NW)
        wh, wl = pair("w", [P, NW, KC, C])
        stage = sb("stage", [P, 2, KC, C])
        ident = sb("ident", [P, P])
        blocks = sb("blocks", [P, P])
        heads = sb("heads", [P, HB])
        boutb = sb("boutb", [P, C])
        bvb = sb("bvb", [P, C])
        bob = sb("bob", [P, C])
        bqk = sb("bqk", [P, 2, KC])
        half_power = sb("half_power", [P, T])
        eps = sb("eps", [P, T])

        xs = sb("x", [P, T, C])
        xb = sb("xb", [P, T, C])
        stats = sb("stats", [P, 2, T, 6])
        mv = sb("mv", [P, 2, T, 2])
        vare = sb("vare", [P, 2, T])
        rstd = sb("rstd", [P, 2, T])
        zn = sb("zn", [P, 2, T, C])
        xTh, xTl = pair("xT", [P, KC, S])
        qm = sb("qm", [P, 2, 2 * C])
        qe = sb("qe", [P, 2, 2 * C])
        q1T = sb("q1T", [P, KC, S])
        k1 = sb("k1", [P, T, C])
        v1 = sb("v1", [P, T, KC, P + 1])
        kvm = sb("kvm", [P, KC, W1])
        den = sb("den", [P, T, KC, HB])
        rden = sb("rden", [P, T, KC, HB])
        o1 = sb("o1", [P, T, C])
        oTh, oTl = pair("oT", [P, KC, S])
        x1 = sb("x1", [P, 2, T, C])
        xr = sb("xr", [P, 2, T, C])
        yTh, yTl = pair("yT", [P, KC, S])
        cs = sb("c", [P, T, C])
        cTh, cTl = pair("cT", [P, KC, S])
        qkf = sb("qkf", [P, 2, KC, S])
        qk = sb("qk", [P, 4, KC, S], F32R)
        vx = sb("vx", [P, 2, T, H, 32])
        ms = sb("mask", [P, 2, T, S])
        Q = sb("Q", [P, H, S], F32R)
        K = sb("K", [P, H, S], F32R)
        sc = sb("sc", [P, 4, T, 2, S])
        nmx = sb("nmx", [P, 4, T, 2])
        PT = sb("PT", [P, 8, 2 * S])
        oS = sb("oS", [P, G, S])
        rd = sb("rd", [P, T, H])
        oN = sb("oN", [P, T, C])
        nTh, nTl = pair("nT", [P, KC, S])
        x2s = sb("x2", [P, T, C])

        pA = ctx.enter_context(nc.psum_tensor("a_pA", [P, 2, 512], F32))
        pS = ctx.enter_context(nc.psum_tensor("a_pS", [P, T, 2, S], F32))
        pP = ctx.enter_context(nc.psum_tensor("a_pP", [P, 2, 512], F32))
        pO = ctx.enter_context(nc.psum_tensor("a_pO", [P, 2, 512], F32))

        small_loaded = sem("small_loaded")
        passed = sem("passed")
        stage_loaded = [sem(f"stage_loaded{i}") for i in range(2)]
        split_hi, split_lo = sem("split_hi"), sem("split_lo")
        pool_set, dve_set, act_set = sem("pool_set"), sem("dve_set"), sem("act_set")
        x_loaded, c_loaded = sem("x_loaded"), sem("c_loaded")
        m_loaded = [sem(f"m_loaded{i}") for i in range(2)]
        stats_step = [sem(f"stats_step{i}") for i in range(2)]
        vare_ready = [sem(f"vare_ready{i}") for i in range(2)]
        rstd_ready = [sem(f"rstd_ready{i}") for i in range(2)]
        zn_ready = [sem(f"zn_ready{i}") for i in range(2)]
        xb_ready, xr_ready = sem("xb_ready"), sem("xr_ready")
        xT_done, xTh_ready, xTl_ready = sem("xT_done"), sem("xTh_ready"), sem("xTl_ready")
        lq_done, lk_done, lv_done = sem("lq_done"), sem("lk_done"), sem("lv_done")
        qm_ready, km_ready = sem("qm_ready"), sem("km_ready")
        qe_ready, ke_ready = sem("qe_ready"), sem("ke_ready")
        q1_ready, k1_ready, v1_ready = sem("q1_ready"), sem("k1_ready"), sem("v1_ready")
        kv_done, kvm_ready = sem("kv_done"), sem("kvm_ready")
        o1_done, den_ready, rden_ready, o1_ready = sem("o1_done"), sem("den_ready"), sem("rden_ready"), sem("o1_ready")
        oT_done, oTh_ready, oTl_ready = sem("oT_done"), sem("oTh_ready"), sem("oTl_ready")
        x1_done, x1_ready = sem("x1_done"), sem("x1_ready")
        yT_done, yTh_ready, yTl_ready = sem("yT_done"), sem("yTh_ready"), sem("yTl_ready")
        cT_done, cTh_ready, cTl_ready = sem("cT_done"), sem("cTh_ready"), sem("cTl_ready")
        cq_done, ck_done, cv_done = sem("cq_done"), sem("ck_done"), sem("cv_done")
        qf_ready, kf_ready = sem("qf_ready"), sem("kf_ready")
        qh_ready, ql_ready, kh_ready, kl_ready = sem("qh_ready"), sem("ql_ready"), sem("kh_ready"), sem("kl_ready")
        vx_ready = sem("vx_ready")
        qk_stored = sem("qk_stored")
        qk_loaded = [sem(f"qk_loaded{i}") for i in range(KC)]
        s_done, s_ready, p_ready = sem("s_done"), sem("s_ready"), sem("p_ready")
        pT_done = sem("pT_done")
        pT_ready = [sem(f"pT_ready{i}") for i in range(2)]
        pv_done, oS_ready = sem("pv_done"), sem("oS_ready")
        nq_done, rd_ready, oN_ready = sem("nq_done"), sem("rd_ready"), sem("oN_ready")
        nT_done, nTh_ready, nTl_ready = sem("nT_done"), sem("nTh_ready"), sem("nTl_ready")
        x2_done, x2_ready, x2_stored = sem("x2_done"), sem("x2_ready"), sem("x2_stored")

        BANK = {"cT": 0, "xT": 1, "yT": 0, "n0": 1, "n1": 0, "cq": 1, "lk": 0, "ck": 1, "lq": 0, "lv": 1,
                "nT": 0, "kv": 1, "x2": 0, "cv": 1, "o0": 0, "o1": 1, "oT": 0, "x1": 1}
        READER = {
            "cT": (cTl_ready, lambda b: b + 1), "xT": (xTl_ready, lambda b: b + 1),
            "yT": (yTl_ready, lambda b: b + 1), "n0": (oN_ready, lambda b: T * b + 1),
            "n1": (oN_ready, lambda b: T * b + 2), "lq": (q1_ready, lambda b: b + 1),
            "lk": (k1_ready, lambda b: b + 1), "cq": (qf_ready, lambda b: KC * (b + 1)),
            "lv": (v1_ready, lambda b: b + 1), "nT": (nTl_ready, lambda b: b + 1),
            "ck": (kf_ready, lambda b: KC * (b + 1)), "kv": (kvm_ready, lambda b: 2 * (b + 1)),
            "x2": (x2_ready, lambda b: b + 1), "cv": (vx_ready, lambda b: b + 1),
            "o0": (o1_ready, lambda b: T * b + 1), "o1": (o1_ready, lambda b: T * b + 2),
            "oT": (oTl_ready, lambda b: b + 1), "x1": (x1_ready, lambda b: b + 1),
        }

        def each_batch(engine, body):
            body(0, 0)
            body(1, 1)
            with engine.Fori(1, B // 2 - 1) as i:
                body(i * 2, 0)
                body(i * 2 + 1, 1)
            body(B - 2, 0)
            body(B - 1, 1)

        def has(b):
            return not isinstance(b, int) or 0 <= b < B

        def rows(dram, b):
            v = dram.rearrange("b (t p) c -> b p t c", p=P)
            return v[b] if isinstance(b, int) else v[bass.ds(b, 1)].rearrange("o p t c -> (o p) t c")

        def bank(name):
            return pA[:, BANK[name], :]

        def halves(name):
            return bank(name).rearrange("p (k t) -> p k t", k=2)

        def heads_of(name):
            return bank(name)[:, 0:KC * W1].rearrange("p (m w) -> p m w", m=KC)

        block = ctx.enter_context(nc.Block())

        @block.sync
        def _(sp):
            def load_x(b):
                wait_apart(sp, zn_ready[0], T * b, passed)
                wait_apart(sp, xb_ready, b, passed)
                sp.dma_start(xs[:], rows(x, b)).then_inc(x_loaded, 16)

            def load_c(b):
                wait_apart(sp, cT_done, b, passed)
                sp.dma_start(cs[:], rows(ctx_in, b)).then_inc(c_loaded, 16)

            def load_mask(b, s):
                wait_apart(sp, s_ready, 2 * H * (b - 1), passed)
                sp.dma_start(ms[:, s], rows(mask, b)).then_inc(m_loaded[s], 16)

            def scratch(b):
                v = qk_dram.rearrange("b f (m p) t -> b p f m t", p=P)
                return v[b] if isinstance(b, int) else v[bass.ds(b, 1)].rearrange("o p f m t -> (o p) f m t")

            def spread(b, part, m):
                v = qk_dram.rearrange("b f (m h d) t -> b f m d h t", m=KC, d=D)
                if isinstance(b, int):
                    return v[b, part, m]
                return v[bass.ds(b, 1), part, m].rearrange("o d h t -> (o d) h t")

            def store_qk(b):
                wait_apart(sp, ql_ready, b + 1, passed)
                wait_apart(sp, kl_ready, b + 1, passed)
                sp.dma_start(scratch(b), qk[:].bitcast(F32)).then_inc(qk_stored, 16)

            def load_qk(b, m):
                wait_apart(sp, qk_stored, 16 * (b + 1), passed)
                wait_apart(sp, s_done, 2 * HP * (b - 1) + HP * (m + 1), passed)
                for tile, parts in ((Q, (0, 1, 0)), (K, (2, 2, 3))):
                    for i, part in enumerate(parts):
                        sp.dma_start(tile[D * i:D * (i + 1), m * HB:(m + 1) * HB, :].bitcast(F32),
                                     spread(b, part, m)).then_inc(qk_loaded[m], 16)

            def store_x2(b):
                wait_apart(sp, x2_ready, b + 1, passed)
                sp.dma_start(rows(x2, b), x2s[:]).then_inc(x2_stored, 16)

            for dst, src in ((ident[:], ident_in), (blocks[:], block_in), (heads[:], heads_in),
                             (boutb[:], b_out[None, :].broadcast_to([P, C])),
                             (bvb[:], bv[None, :].broadcast_to([P, C])), (bob[:], bo[None, :].broadcast_to([P, C])),
                             (bqk[:, 0], bq), (bqk[:, 1], bk)):
                sp.dma_start(dst, src).then_inc(small_loaded, 16)
            load_x(0)
            load_c(0)
            wT = [wqkvT[:, 0:C], wqkvT[:, C:2 * C], wqkvT[:, 2 * C:3 * C], woutT, wqT, wkT, wvT, woT]
            for n, w in enumerate(wT):
                wait_apart(sp, split_lo, n - 1, passed)
                sp.dma_start(stage[:, n % 2], w.rearrange("(k p) n -> p k n", p=P)).then_inc(stage_loaded[n % 2], 16)
            load_mask(0, 0)
            load_mask(1, 1)
            load_x(1)
            load_c(1)
            sp.wait_ge(pool_set, 4)
            store_qk(0)
            load_qk(0, 0)
            load_qk(0, 1)

            def body(b, s):
                if s == 0 and has(b + 2):
                    load_x(b + 2)
                if has(b + 2):
                    load_c(b + 2)
                if s == 0 and has(b + 3):
                    load_x(b + 3)
                if has(b + 1):
                    store_qk(b + 1)
                    load_qk(b + 1, 0)
                if has(b - 1):
                    store_x2(b - 1)
                if has(b + 1):
                    load_qk(b + 1, 1)
                if has(b + 2):
                    load_mask(b + 2, s)

            each_batch(sp, body)
            store_x2(B - 1)
            sp.wait_ge(x2_stored, 16 * B)

        @block.gpsimd
        def _(pool):
            nc.gpsimd.memset(half_power[:], -0.5).then_inc(pool_set, 1)
            nc.gpsimd.memset(eps[:], LN_EPS).then_inc(pool_set, 1)
            nc.gpsimd.memset(Q[:].bitcast(F32), 0.0).then_inc(pool_set, 1)
            nc.gpsimd.memset(K[:].bitcast(F32), 0.0).then_inc(pool_set, 1)
            pool.wait_ge(pool_set, 4)
            pool.wait_ge(small_loaded, 16 * 8)

            def rsqrt(b, i):
                pool.wait_ge(stats_step[i], 2 * T * (b + 1))
                wait(pool, zn_ready[i], T * b)
                nc.gpsimd.tensor_tensor(out=vare[:, i], in0=mv[:, i, :, 1], in1=eps[:],
                                        op=ALU.add).then_inc(vare_ready[i], 1)
                pool.wait_ge(vare_ready[i], b + 1)
                nc.gpsimd.tensor_tensor(out=rstd[:, i], in0=vare[:, i], in1=half_power[:],
                                        op=ALU.pow).then_inc(rstd_ready[i], 1)

            def add_bout(b):
                pool.wait_ge(x_loaded, 16 * (b + 1))
                wait(pool, x1_ready, b)
                nc.gpsimd.tensor_tensor(out=xb[:], in0=xs[:], in1=boutb[:, None, :].broadcast_to([P, T, C]),
                                        op=ALU.add).then_inc(xb_ready, 1)

            def add_bo(b, s):
                pool.wait_ge(x1_ready, b + 1)
                wait(pool, x2_ready, b - 1)
                nc.gpsimd.tensor_tensor(out=xr[:, s], in0=x1[:, s], in1=bob[:, None, :].broadcast_to([P, T, C]),
                                        op=ALU.add).then_inc(xr_ready, 1)

            for b in range(2):
                rsqrt(b, 0)
                add_bout(b)
            rsqrt(0, 1)
            add_bo(0, 0)

            def body(b, s):
                if has(b + 1):
                    rsqrt(b + 1, 1)
                if has(b + 2):
                    rsqrt(b + 2, 0)
                if has(b + 2):
                    add_bout(b + 2)
                if has(b + 1):
                    add_bo(b + 1, 1 - s)

            each_batch(pool, body)

        @block.scalar
        def _(act):
            act.wait_ge(small_loaded, 16 * 8)

            def high_part(done, ready, low_ready, name, out, b, reader):
                act.wait_ge(done, b + 1)
                for used, n in reader:
                    wait(act, used, n)
                nc.scalar.copy(out[:], halves(name)).then_inc(ready, 1)

            def x_high(b):
                high_part(xT_done, xTh_ready, xTl_ready, "xT", xTh, b, [(lv_done, b)])

            def exp_q(b):
                act.wait_ge(qm_ready, b + 1)
                wait(act, q1_ready, b)
                nc.scalar.activation(qe[:, 0], qm[:, 0], ACT.Exp).then_inc(qe_ready, 1)

            def exp_k(b):
                act.wait_ge(km_ready, b + 1)
                wait(act, k1_ready, b)
                nc.scalar.activation(qe[:, 1], qm[:, 1], ACT.Exp).then_inc(ke_ready, 1)

            def copy_v1(b):
                act.wait_ge(lv_done, b + 1)
                wait(act, kv_done, b)
                nc.scalar.copy(v1[:, :, :, 0:P],
                               bank("lv").rearrange("p (t m c) -> p t m c", t=T, m=KC)).then_inc(v1_ready, 1)

            def o_high(b):
                high_part(oT_done, oTh_ready, oTl_ready, "oT", oTh, b, [(x1_done, b)])

            def y_high(b):
                high_part(yT_done, yTh_ready, yTl_ready, "yT", yTh, b, [(cq_done, b)])

            def c_high(b):
                high_part(cT_done, cTh_ready, cTl_ready, "cT", cTh, b, [(cv_done, b)])

            def n_high(b):
                high_part(nT_done, nTh_ready, nTl_ready, "nT", nTh, b, [(x2_done, b)])

            def biased(b, i, name, done, ready, low_ready, scale):
                act.wait_ge(done, b + 1)
                wait(act, low_ready, b)
                for m in range(KC):
                    nc.scalar.activation(qkf[:, i, m], halves(name)[:, m], ACT.Identity, bias=bqk[:, i, m:m + 1],
                                         scale=scale).then_inc(ready, 1)

            def cross_q(b):
                biased(b, 0, "cq", cq_done, qf_ready, ql_ready, SCALE)

            def cross_k(b):
                biased(b, 1, "ck", ck_done, kf_ready, kl_ready, 1.0)

            def exps(b, hp):
                for t in range(T):
                    for j in range(2):
                        act.wait_ge(s_ready, 2 * H * b + 4 * hp + 2 * t + j + 1)
                        nc.scalar.activation(sc[:, hp % 4, t, j], sc[:, hp % 4, t, j], ACT.Exp,
                                             bias=nmx[:, hp % 4, t, j:j + 1], scale=-1.0).then_inc(p_ready, 1)

            def take_pT(b, hp):
                h = 2 * hp
                act.wait_ge(pT_done, H * b + h + 1)
                wait(act, pv_done, G * b + h // 4 - 1)
                nc.scalar.copy(PT[:, h % 8], pP[:, 0]).then_inc(pT_ready[0], 1)

            def take_pO(b, g):
                act.wait_ge(pv_done, G * b + g + 1)
                wait(act, nq_done, T * b)
                nc.scalar.copy(oS[:, g], pO[:, g % 2, 0:S]).then_inc(oS_ready, 1)

            nc.scalar.mul(bqk[:, 0], bqk[:, 0], SCALE).then_inc(act_set, 1)
            act.wait_ge(act_set, 1)
            for b in range(2):
                x_high(b)
                exp_k(b)
                exp_q(b)
                copy_v1(b)
                o_high(b)
            c_high(0)
            y_high(0)
            cross_q(0)
            cross_k(0)

            def body(b, s):
                A, V, F = b + 2, b + 1, b - 1
                exps(b, 0)
                if has(F):
                    take_pT(F, 7)
                if has(V):
                    c_high(V)
                exps(b, 1)
                if has(F):
                    take_pO(F, 3)
                take_pT(b, 0)
                if has(A):
                    x_high(A)
                if has(V):
                    y_high(V)
                exps(b, 2)
                take_pT(b, 1)
                if has(V):
                    cross_q(V)
                if has(A):
                    exp_k(A)
                exps(b, 3)
                take_pO(b, 0)
                take_pT(b, 2)
                if has(V):
                    cross_k(V)
                if has(A):
                    exp_q(A)
                    copy_v1(A)
                exps(b, 4)
                take_pT(b, 3)
                if has(F):
                    n_high(F)
                exps(b, 5)
                take_pO(b, 1)
                take_pT(b, 4)
                exps(b, 6)
                take_pT(b, 5)
                if has(A):
                    o_high(A)
                exps(b, 7)
                take_pO(b, 2)
                take_pT(b, 6)

            each_batch(act, body)
            take_pT(B - 1, 7)
            take_pO(B - 1, 3)
            n_high(B - 1)

        @block.vector
        def _(dve):
            nc.vector.memset(v1[:], 1.0).then_inc(dve_set, 1)
            nc.vector.memset(vx[:], 0.0).then_inc(dve_set, 1)
            dve.wait_ge(dve_set, 2)
            for n in range(NW):
                dve.wait_ge(stage_loaded[n % 2], 16 * (n // 2 + 1))
                nc.vector.tensor_copy(wh[:, n], stage[:, n % 2]).then_inc(split_hi, 1)
                dve.wait_ge(split_hi, n + 1)
                nc.vector.tensor_tensor(out=wl[:, n], in0=stage[:, n % 2], in1=wh[:, n],
                                        op=ALU.subtract).then_inc(split_lo, 1)
            nc.vector.memset(vx[:, :, :, :, D:D + 1], 1.0).then_inc(dve_set, 1)
            dve.wait_ge(dve_set, 3)
            dve.wait_ge(small_loaded, 16 * 8)

            def moments(b, i, src):
                wait(dve, zn_ready[i], T * b)
                for t in range(T):
                    nc.vector.bn_stats(stats[:, i, t], src[:, t]).then_inc(stats_step[i], 1)
                wait_apart(dve, stats_step[i], 2 * T * b + T, passed)
                for t in range(T):
                    nc.vector.bn_aggr(mv[:, i, t], stats[:, i, t]).then_inc(stats_step[i], 1)

            def layernorm(b, i, src, transposed):
                dve.wait_ge(rstd_ready[i], b + 1)
                wait(dve, transposed, b)
                for t in range(T):
                    nc.vector.tensor_scalar(zn[:, i, t], src[:, t], mv[:, i, t, 0:1], rstd[:, i, t:t + 1],
                                            ALU.subtract, ALU.mult).then_inc(zn_ready[i], 1)

            def moments_x(b):
                dve.wait_ge(x_loaded, 16 * (b + 1))
                moments(b, 0, xs)

            def norm_x(b):
                layernorm(b, 0, xs, xT_done)

            def moments_x1(b, s):
                dve.wait_ge(x1_ready, b + 1)
                moments(b, 1, x1[:, s])

            def norm_x1(b, s):
                layernorm(b, 1, x1[:, s], yT_done)

            def low_part(high_ready, ready, name, high, low, b):
                dve.wait_ge(high_ready, b + 1)
                nc.vector.tensor_tensor(out=low[:], in0=halves(name), in1=high[:],
                                        op=ALU.subtract).then_inc(ready, 1)

            def x_low(b):
                low_part(xTh_ready, xTl_ready, "xT", xTh, xTl, b)

            def o_low(b):
                low_part(oTh_ready, oTl_ready, "oT", oTh, oTl, b)

            def y_low(b):
                low_part(yTh_ready, yTl_ready, "yT", yTh, yTl, b)

            def c_low(b):
                low_part(cTh_ready, cTl_ready, "cT", cTh, cTl, b)

            def n_low(b):
                low_part(nTh_ready, nTl_ready, "nT", nTh, nTl, b)

            def negative(b, i, name, done, exp_ready, ready):
                dve.wait_ge(done, b + 1)
                wait(dve, exp_ready, b)
                nc.vector.tensor_scalar(qm[:, i], bank(name), 0.0, 1.0, ALU.min, ALU.mult).then_inc(ready, 1)

            def feature(b, i, name, exp_ready, used, out, ready):
                dve.wait_ge(exp_ready, b + 1)
                wait(dve, used, b)
                nc.vector.scalar_tensor_tensor(out=out, in0=bank(name), scalar=0.0, in1=qe[:, i], op0=ALU.max,
                                               op1=ALU.add).then_inc(ready, 1)

            def neg_q(b):
                negative(b, 0, "lq", lq_done, qe_ready, qm_ready)

            def neg_k(b):
                negative(b, 1, "lk", lk_done, ke_ready, km_ready)

            def feat_q(b):
                wait(dve, o1_done, T * b)
                feature(b, 0, "lq", qe_ready, o1_done, q1T[:].rearrange("p k t -> p (k t)"), q1_ready)

            def feat_k(b):
                feature(b, 1, "lk", ke_ready, kv_done, k1[:].rearrange("p t c -> p (t c)"), k1_ready)

            def mask_kv(b):
                dve.wait_ge(kv_done, b + 1)
                wait(dve, o1_done, T * b)
                kv = bank("kv")[:, 0:KC * (P + 1)].rearrange("p (m w) -> p m w", m=KC)
                nc.vector.tensor_tensor(out=kvm[:, :, 0:P], in0=kv[:, :, 0:P],
                                        in1=blocks[:, None, :].broadcast_to([P, KC, P]),
                                        op=ALU.mult).then_inc(kvm_ready, 1)
                nc.vector.tensor_tensor(out=kvm[:, :, P:W1], in0=kv[:, :, P:P + 1].broadcast_to([P, KC, HB]),
                                        in1=heads[:, None, :].broadcast_to([P, KC, HB]),
                                        op=ALU.mult).then_inc(kvm_ready, 1)

            def divide(b):
                for t in range(T):
                    dve.wait_ge(o1_done, T * b + t + 1)
                    nc.vector.tensor_scalar(den[:, t], heads_of(f"o{t}")[:, :, P:W1], DEN_EPS, 1.0, ALU.add,
                                            ALU.mult).then_inc(den_ready, 1)
                wait(dve, o1_ready, T * b)
                dve.wait_ge(den_ready, T * (b + 1))
                nc.vector.reciprocal(rden[:], den[:]).then_inc(rden_ready, 1)
                dve.wait_ge(rden_ready, b + 1)
                wait(dve, oT_done, b)
                for t in range(T):
                    nc.vector.tensor_tensor(
                        out=o1[:, t].rearrange("p (m h d) -> p m h d", m=KC, d=D),
                        in0=heads_of(f"o{t}")[:, :, 0:P].rearrange("p m (h d) -> p m h d", d=D),
                        in1=rden[:, t][:, :, :, None].broadcast_to([P, KC, HB, D]), op=ALU.mult,
                    ).then_inc(o1_ready, 1)

            def residual_1(b, s):
                dve.wait_ge(x1_done, b + 1)
                dve.wait_ge(xb_ready, b + 1)
                wait(dve, xr_ready, b - 1)
                nc.vector.tensor_tensor(out=x1[:, s], in0=bank("x1").rearrange("p (t c) -> p t c", t=T), in1=xb[:],
                                        op=ALU.add).then_inc(x1_ready, 1)

            def split_qk(b, i, float_ready, high_ready, ready):
                dve.wait_ge(float_ready, KC * (b + 1))
                wait(dve, qk_stored, 16 * b)
                nc.vector.tensor_copy(qk[:, 2 * i], qkf[:, i]).then_inc(high_ready, 1)
                dve.wait_ge(high_ready, b + 1)
                nc.vector.tensor_tensor(out=qk[:, 2 * i + 1], in0=qkf[:, i], in1=qk[:, 2 * i],
                                        op=ALU.subtract).then_inc(ready, 1)

            def split_q(b):
                split_qk(b, 0, qf_ready, qh_ready, ql_ready)

            def split_k(b):
                split_qk(b, 1, kf_ready, kh_ready, kl_ready)

            def cross_v(b, s):
                dve.wait_ge(cv_done, b + 1)
                wait(dve, pv_done, G * (b - 1))
                nc.vector.tensor_tensor(out=vx[:, s, :, :, 0:D],
                                        in0=bank("cv").rearrange("p (t h d) -> p t h d", t=T, d=D),
                                        in1=bvb[:].rearrange("p (h d) -> p h d", d=D)[:, None].broadcast_to(
                                            [P, T, H, D]), op=ALU.add).then_inc(vx_ready, 1)

            def scores(b, s, hp):
                if hp == 0:
                    dve.wait_ge(m_loaded[s], 16 * (b // 2 + 1))
                wait(dve, pT_done, H * b + 2 * (hp - 3))
                for t in range(T):
                    wait_apart(dve, s_done, 2 * HP * b + 2 * hp + t + 1, passed)
                    for j in range(2):
                        nc.vector.tensor_tensor_reduce(
                            out=sc[:, hp % 4, t, j], in0=pS[:, t, j], in1=ms[:, s, t], scale=-1.0,
                            scalar=BIG, op0=ALU.add, op1=ALU.min,
                            accum_out=nmx[:, hp % 4, t, j:j + 1]).then_inc(s_ready, 1)

            def take_pT(b, hp):
                h = 2 * hp + 1
                dve.wait_ge(pT_done, H * b + h + 1)
                wait(dve, pv_done, G * b + h // 4 - 1)
                nc.vector.tensor_copy(PT[:, h % 8], pP[:, 1]).then_inc(pT_ready[1], 1)

            def normalise(b):
                for t in range(T):
                    dve.wait_ge(nq_done, T * b + t + 1)
                    o = bank(f"n{t}").rearrange("p (h w) -> p h w", w=32)
                    wait(dve, oN_ready, T * b)
                    nc.vector.reciprocal(rd[:, t], o[:, :, D]).then_inc(rd_ready, 1)
                    dve.wait_ge(rd_ready, T * b + t + 1)
                    wait(dve, nT_done, b)
                    nc.vector.tensor_tensor(out=oN[:, t].rearrange("p (h d) -> p h d", d=D), in0=o[:, :, 0:D],
                                            in1=rd[:, t][:, :, None].broadcast_to([P, H, D]),
                                            op=ALU.mult).then_inc(oN_ready, 1)

            def residual_2(b, s):
                dve.wait_ge(x2_done, b + 1)
                dve.wait_ge(xr_ready, b + 1)
                wait(dve, x2_stored, 16 * b)
                nc.vector.tensor_tensor(out=x2s[:], in0=bank("x2").rearrange("p (t c) -> p t c", t=T),
                                        in1=xr[:, s], op=ALU.add).then_inc(x2_ready, 1)

            for b in range(2):
                moments_x(b)
                norm_x(b)
                x_low(b)
                neg_k(b)
                feat_k(b)
                neg_q(b)
                feat_q(b)
                mask_kv(b)
                divide(b)
                o_low(b)
                residual_1(b, b)
            c_low(0)
            moments_x1(0, 0)
            norm_x1(0, 0)
            y_low(0)
            split_q(0)
            split_k(0)
            cross_v(0, 0)
            scores(0, 0, 0)

            def body(b, s):
                A, V, F = b + 2, b + 1, b - 1
                scores(b, s, 1)
                if has(F):
                    take_pT(F, 7)
                if has(V):
                    moments_x1(V, 1 - s)
                if has(A):
                    moments_x(A)
                if has(V):
                    norm_x1(V, 1 - s)
                    c_low(V)
                if has(A):
                    norm_x(A)
                scores(b, s, 2)
                take_pT(b, 0)
                if has(A):
                    x_low(A)
                if has(V):
                    y_low(V)
                scores(b, s, 3)
                take_pT(b, 1)
                if has(F):
                    normalise(F)
                if has(A):
                    neg_k(A)
                if has(V):
                    split_q(V)
                if has(A):
                    feat_k(A)
                scores(b, s, 4)
                take_pT(b, 2)
                if has(A):
                    neg_q(A)
                if has(V):
                    split_k(V)
                if has(A):
                    feat_q(A)
                scores(b, s, 5)
                take_pT(b, 3)
                if has(F):
                    n_low(F)
                if has(A):
                    mask_kv(A)
                scores(b, s, 6)
                take_pT(b, 4)
                if has(F):
                    residual_2(F, 1 - s)
                if has(V):
                    cross_v(V, 1 - s)
                if has(A):
                    divide(A)
                scores(b, s, 7)
                take_pT(b, 5)
                if has(A):
                    o_low(A)
                if has(V):
                    scores(V, 1 - s, 0)
                take_pT(b, 6)
                if has(A):
                    residual_1(A, s)

            each_batch(dve, body)
            take_pT(B - 1, 7)
            normalise(B - 1)
            n_low(B - 1)
            residual_2(B - 1, 1)

        @block.tensor
        def _(pe):
            occupant = [None, None]

            def take_bank(name, b):
                r = BANK[name]
                if occupant[r] is not None:
                    before, of = occupant[r]
                    semaphore, count = READER[before]
                    pe.wait_ge(semaphore, count(of))
                occupant[r] = (name, b)
                return pA[:, r, :]

            def product(out_ap, terms):
                for i, (lhsT, rhs) in enumerate(terms):
                    ins = nc.tensor.matmul(out_ap, lhsT, rhs, start=(i == 0), stop=(i == len(terms) - 1))
                return ins

            def transposed(name, b, src, done, ready):
                for semaphore, n in ready:
                    pe.wait_ge(semaphore, n)
                out = take_bank(name, b)
                for k in range(KC):
                    for t in range(T):
                        ins = nc.tensor.transpose(out[:, k * S + t * P:k * S + (t + 1) * P],
                                                  src[:, t, k * P:(k + 1) * P], ident[:])
                ins.then_inc(done, 1)

            def to_features(name, b, w, hi, lo, done, ready):
                for semaphore, n in ready:
                    pe.wait_ge(semaphore, n)
                out = take_bank(name, b)
                for m in range(KC):
                    cols = slice(m * P, (m + 1) * P)
                    ins = product(out[:, m * S:(m + 1) * S],
                                  [(a[:, w, k, cols], z[:, k]) for k in range(KC)
                                   for a, z in ((wh, hi), (wl, hi), (wh, lo))])
                ins.then_inc(done, 1)

            def to_tokens(name, b, w, hi, lo, done, ready):
                for semaphore, n in ready:
                    pe.wait_ge(semaphore, n)
                out = take_bank(name, b)
                for t in range(T):
                    toks = slice(t * P, (t + 1) * P)
                    ins = product(out[:, t * C:(t + 1) * C],
                                  [(z[:, k, toks], a[:, w, k]) for k in range(KC)
                                   for a, z in ((wh, hi), (wl, hi), (wh, lo))])
                ins.then_inc(done, 1)

            def x_T(b):
                transposed("xT", b, zn[:, 0], xT_done, [(zn_ready[0], T * (b + 1))])

            def lin_q(b):
                to_features("lq", b, LQ, xTh, xTl, lq_done, [(xTl_ready, b + 1)])

            def lin_k(b):
                to_tokens("lk", b, LK, xTh, xTl, lk_done, [(xTl_ready, b + 1)])

            def lin_v(b):
                to_tokens("lv", b, LV, xTh, xTl, lv_done, [(xTl_ready, b + 1)])

            def lin_kv(b):
                pe.wait_ge(k1_ready, b + 1)
                pe.wait_ge(v1_ready, b + 1)
                out = take_bank("kv", b)
                for m in range(KC):
                    ins = product(out[:, m * (P + 1):(m + 1) * (P + 1)],
                                  [(k1[:, t, m * P:(m + 1) * P], v1[:, t, m]) for t in range(T)])
                ins.then_inc(kv_done, 1)

            def lin_o(b):
                pe.wait_ge(q1_ready, b + 1)
                pe.wait_ge(kvm_ready, 2 * (b + 1))
                for t in range(T):
                    out = take_bank(f"o{t}", b)
                    for m in range(KC):
                        ins = nc.tensor.matmul(out[:, m * W1:(m + 1) * W1], q1T[:, m, t * P:(t + 1) * P],
                                               kvm[:, m], start=True, stop=True)
                    ins.then_inc(o1_done, 1)

            def o_T(b):
                transposed("oT", b, o1, oT_done, [(o1_ready, T * (b + 1))])

            def lin_out(b):
                to_tokens("x1", b, LO, oTh, oTl, x1_done, [(oTl_ready, b + 1)])

            def y_T(b):
                transposed("yT", b, zn[:, 1], yT_done, [(zn_ready[1], T * (b + 1))])

            def c_T(b):
                transposed("cT", b, cs, cT_done, [(c_loaded, 16 * (b + 1))])

            def cross_q(b):
                to_features("cq", b, CQ, yTh, yTl, cq_done, [(yTl_ready, b + 1)])

            def cross_k(b):
                to_features("ck", b, CK, cTh, cTl, ck_done, [(cTl_ready, b + 1)])

            def cross_v(b):
                to_tokens("cv", b, CV, cTh, cTl, cv_done, [(cTl_ready, b + 1)])

            def scores(b, hp):
                if hp % (HP // KC) == 0:
                    pe.wait_ge(qk_loaded[hp // (HP // KC)], 16 * 6 * (b + 1))
                for t in range(T):
                    wait(pe, s_ready, 2 * H * b + 4 * (hp - 1) + 2 * t + 2)
                    for j in range(2):
                        h = 2 * hp + j
                        ins = nc.tensor.matmul(pS[:, t, j], Q[:, h, t * P:(t + 1) * P], K[:, h], start=True,
                                               stop=True)
                    ins.then_inc(s_done, 1)

            def prob_T(b, hp):
                pe.wait_ge(p_ready, 2 * H * b + 4 * hp + 4)
                for j in range(2):
                    wait(pe, pT_ready[j], HP * b + hp)
                    for k in range(T):
                        for t in range(T):
                            ins = nc.tensor.transpose(pP[:, j, k * S + t * P:k * S + (t + 1) * P],
                                                      sc[:, hp % 4, t, j, k * P:(k + 1) * P], ident[:])
                    ins.then_inc(pT_done, 1)

            def values(b, s, g):
                pe.wait_ge(pT_ready[0], HP * b + 2 * g + 2)
                pe.wait_ge(pT_ready[1], HP * b + 2 * g + 2)
                pe.wait_ge(vx_ready, b + 1)
                wait(pe, oS_ready, G * b + g - 1)
                for k in range(T):
                    for j in range(4):
                        h = 4 * g + j
                        ins = nc.tensor.matmul(pO[32 * j:32 * j + 32, g % 2, 0:S], vx[:, s, k, h],
                                               PT[:, h % 8, k * S:(k + 1) * S], start=(k == 0), stop=(k == T - 1))
                ins.then_inc(pv_done, 1)

            def outputs_back(b):
                pe.wait_ge(oS_ready, G * (b + 1))
                for t in range(T):
                    out = take_bank(f"n{t}", b)
                    for g in range(G):
                        ins = nc.tensor.transpose(out[:, g * P:(g + 1) * P], oS[:, g, t * P:(t + 1) * P], ident[:])
                    ins.then_inc(nq_done, 1)

            def n_T(b):
                transposed("nT", b, oN, nT_done, [(oN_ready, T * (b + 1))])

            def cross_out(b):
                to_tokens("x2", b, CO, nTh, nTl, x2_done, [(nTl_ready, b + 1)])

            pe.wait_ge(small_loaded, 16 * 8)
            pe.wait_ge(pool_set, 4)
            pe.wait_ge(dve_set, 3)
            pe.wait_ge(split_lo, NW)
            for b in range(2):
                x_T(b)
                lin_k(b)
                lin_q(b)
                lin_v(b)
                lin_kv(b)
                lin_o(b)
                o_T(b)
                lin_out(b)
            c_T(0)
            y_T(0)
            cross_q(0)
            cross_k(0)
            cross_v(0)
            scores(0, 0)

            def body(b, s):
                A, V, F = b + 2, b + 1, b - 1
                if not isinstance(b, int) or b not in (0, B - 1):
                    occupant[:] = [("oT", b + 1), ("x1", b + 1)]
                scores(b, 1)
                if has(F):
                    prob_T(F, 7)
                if has(V):
                    c_T(V)
                scores(b, 2)
                if has(F):
                    values(F, 1 - s, 3)
                prob_T(b, 0)
                if has(A):
                    x_T(A)
                if has(V):
                    y_T(V)
                scores(b, 3)
                prob_T(b, 1)
                if has(F):
                    outputs_back(F)
                if has(V):
                    cross_q(V)
                if has(A):
                    lin_k(A)
                scores(b, 4)
                values(b, s, 0)
                prob_T(b, 2)
                if has(V):
                    cross_k(V)
                if has(A):
                    lin_q(A)
                    lin_v(A)
                scores(b, 5)
                prob_T(b, 3)
                if has(F):
                    n_T(F)
                if has(A):
                    lin_kv(A)
                scores(b, 6)
                values(b, s, 1)
                prob_T(b, 4)
                if has(F):
                    cross_out(F)
                if has(V):
                    cross_v(V)
                if has(A):
                    lin_o(A)
                scores(b, 7)
                prob_T(b, 5)
                if has(A):
                    o_T(A)
                if has(V):
                    scores(V, 0)
                values(b, s, 2)
                prob_T(b, 6)
                if has(A):
                    lin_out(A)

            each_batch(pe, body)
            prob_T(B - 1, 7)
            values(B - 1, 1, 3)
            outputs_back(B - 1)
            n_T(B - 1)
            cross_out(B - 1)


def build_moe(nc, x2, ident_in, tri_in, rW1, rb1, rW2, rb2, We1, be1, We2, be2, out):
    B, S, C = x2.shape
    E, _, HID = We1.shape
    RH = rW1.shape[1]
    T = S // P
    KC = C // P
    KH = HID // P
    KR = RH // P
    U = KH // 2
    with ExitStack() as ctx:
        def sb(name, shape, dt=F32):
            return ctx.enter_context(nc.sbuf_tensor("m_" + name, shape, dt))

        def sem(name):
            return ctx.enter_context(nc.semaphore("m_" + name))

        w1h, w1l = (sb(f"w1{p}", [P, E, KC, HID], F32R) for p in "hl")
        w2h, w2l = (sb(f"w2{p}", [P, E, KH, C], F32R) for p in "hl")
        r1h, r1l = (sb(f"r1{p}", [P, KC, RH], F32R) for p in "hl")
        r2 = sb("r2", [P, KR, 32])
        b1 = sb("b1", [P, E, KH])
        rb1s = sb("rb1", [P, KR])
        rb2s = sb("rb2", [P, E])
        b2s = sb("b2", [P, E, C])
        ident = sb("ident", [P, P])
        tri = sb("tri", [P, E, E])
        x = sb("x", [P, 2, T, C])
        zn = sb("zn", [P, T, C])
        zTh, zTl = (sb(f"zT{p}", [P, 2, KC, S], F32R) for p in "hl")
        stats = sb("stats", [P, T, 6])
        mv = sb("mv", [P, T, 2])
        vare = sb("vare", [P, T])
        half_power = sb("half_power", [P, T])
        eps = sb("eps", [P, T])
        rstd = sb("rstd", [P, T])
        rh = sb("rh", [P, KR, S])
        lgT = sb("lgT", [P, S])
        lg = sb("lg", [P, T, E])
        rt = sb("rt", [P, 4, T, E])
        rs = sb("rs", [P, 4, T])
        cmpg = sb("cmpg", [P, T, E, E])
        cmpe = sb("cmpe", [P, T, E, E])
        gate = sb("gate", [P, 2, T, E])
        h = sb("h", [P, 2, 2, S])
        hh, hl = (sb(f"h{p}", [P, 2, KH, S], F32R) for p in "hl")
        acc = sb("acc", [P, 2, T, C])

        pF = ctx.enter_context(nc.psum_tensor("m_pF", [P, 2, 512], F32))
        pH = ctx.enter_context(nc.psum_tensor("m_pH", [P, U, 512], F32))
        pY = ctx.enter_context(nc.psum_tensor("m_pY", [P, T, 512], F32))

        small_loaded = sem("small_loaded")
        passed = sem("passed")
        stage_loaded = [sem(f"stage_loaded{i}") for i in range(2)]
        split_hi = sem("split_hi")
        split_lo = sem("split_lo")
        x_loaded = [sem(f"x_loaded{i}") for i in range(2)]
        stats_step = sem("stats_step")
        vare_ready = sem("vare_ready")
        power_set = sem("power_set")
        rstd_ready = sem("rstd_ready")
        zn_ready = sem("zn_ready")
        zT_done = sem("zT_done")
        zTh_ready = sem("zTh_ready")
        zTl_ready = sem("zTl_ready")
        rh_done = sem("rh_done")
        rh_ready = sem("rh_ready")
        lgT_done = sem("lgT_done")
        lgT_ready = sem("lgT_ready")
        lg_done = sem("lg_done")
        lg_ready = sem("lg_ready")
        rt_step = sem("rt_step")
        ex_ready = sem("ex_ready")
        gate_ready = sem("gate_ready")
        r2_zeroed = sem("r2_zeroed")
        hid_done = sem("hid_done")
        h_ready = sem("h_ready")
        hh_ready = sem("hh_ready")
        hl_ready = sem("hl_ready")
        y_done = sem("y_done")
        acc_step = [sem(f"acc_step{t}") for t in range(T)]
        stored = [sem(f"stored{i}") for i in range(2)]

        pieces = []
        r1v = rW1.rearrange("(k p) n -> p k n", p=P)
        pieces.append((r1v, r1h[:], r1l[:]))
        w1v = We1.rearrange("e (k p) n -> p e k n", p=P)
        w2v = We2.rearrange("e (k p) n -> p e k n", p=P)
        for e in range(E):
            for k in range(KC):
                pieces.append((w1v[:, e, k:k + 1], w1h[:, e, k:k + 1], w1l[:, e, k:k + 1]))
        for e in range(E):
            for k in range(0, KH, U):
                pieces.append((w2v[:, e, k:k + U], w2h[:, e, k:k + U], w2l[:, e, k:k + U]))

        def staged(n):
            inner = pieces[n][0].shape[-1]
            a = (h, acc)[n % 2]
            return a[:].rearrange("p a b c -> p (a b c)").rearrange("p (k n) -> p k n", n=inner)

        xv = x2.rearrange("b (t p) c -> b p t c", p=P)
        ov = out.rearrange("b (t p) c -> b p t c", p=P)
        LN_STEPS = 2 * T
        RT_STEPS = 11
        ACC_STEPS = 2 * E

        def each_batch(engine, body):
            body(0, 0)
            body(1, 1)
            with engine.Fori(1, B // 2 - 1) as i:
                body(i * 2, 0)
                body(i * 2 + 1, 1)
            body(B - 2, 0)
            body(B - 1, 1)

        def last(b):
            return isinstance(b, int) and b == B - 1

        def first(b):
            return isinstance(b, int) and b == 0

        def half(b):
            return b // 2

        block = ctx.enter_context(nc.Block())

        @block.sync
        def _(sp):
            def load_x(b, s):
                wait_apart(sp, acc_step[T - 1], ACC_STEPS * (b - 2) + E, passed)
                src = xv[b] if isinstance(b, int) else xv[bass.ds(b, 1)].rearrange("o p t c -> (o p) t c")
                sp.dma_start(x[:, s], src).then_inc(x_loaded[s], 16)

            sp.dma_start(b1[:], be1).then_inc(small_loaded, 16)
            sp.dma_start(rb1s[:], rb1).then_inc(small_loaded, 16)
            sp.dma_start(rb2s[:], rb2[None, :].broadcast_to([P, E])).then_inc(small_loaded, 16)
            sp.dma_start(b2s[:], be2[None, :, :].broadcast_to([P, E, C])).then_inc(small_loaded, 16)
            sp.dma_start(ident[:], ident_in).then_inc(small_loaded, 16)
            sp.dma_start(tri[:], tri_in).then_inc(small_loaded, 16)
            sp.wait_ge(r2_zeroed, 1)
            sp.dma_start(r2[:, :, 0:E], rW2.rearrange("(k p) n -> p k n", p=P)).then_inc(small_loaded, 16)
            load_x(0, 0)
            load_x(1, 1)
            for n, (src, _, _) in enumerate(pieces):
                wait_apart(sp, split_lo, n - 1, passed)
                sp.dma_start(staged(n), src).then_inc(stage_loaded[n % 2], 16)

            def body(b, s):
                if not (isinstance(b, int) and b >= B - 2):
                    load_x(b + 2, s)
                for t in range(T):
                    wait_apart(sp, acc_step[t], ACC_STEPS * (b + 1), passed)
                dst = ov[b] if isinstance(b, int) else ov[bass.ds(b, 1)].rearrange("o p t c -> (o p) t c")
                sp.dma_start(dst, acc[:, s]).then_inc(stored[s], 16)

            each_batch(sp, body)
            for s in range(2):
                sp.wait_ge(stored[s], 16 * (B // 2))

        @block.scalar
        def _(act):
            act.wait_ge(small_loaded, 16 * 7)

            def front_zT(b, s):
                act.wait_ge(zT_done, b + 1)
                wait(act, hid_done, U * E * (b - 2) + U * E)
                wait(act, rh_done, 2 * (b - 2) + 2)
                nc.scalar.copy(zTh[:, s], pF[:, 0].rearrange("p (k t) -> p k t", k=KC)).then_inc(zTh_ready, 1)

            def front_rh(b, s):
                for r in range(KR):
                    if r % 2 == 0:
                        act.wait_ge(rh_done, 2 * b + r // 2 + 1)
                    if r == 0:
                        wait(act, lgT_done, b)
                    nc.scalar.activation(rh[:, r], pF[:, (r // 2 + 1) % 2, (r % 2) * S:(r % 2 + 1) * S],
                                         ACT.Gelu, bias=rb1s[:, r:r + 1]).then_inc(rh_ready, 1)

            def gelu(b, s, e):
                for u in range(U):
                    n = U * E * b + U * e + u
                    act.wait_ge(hid_done, n + 1)
                    wait(act, hl_ready, n - 1)
                    for j in range(2):
                        nc.scalar.activation(h[:, u % 2, j], pH[:, u, j * S:(j + 1) * S], ACT.Gelu,
                                             bias=b1[:, e, 2 * u + j:2 * u + j + 1]).then_inc(h_ready, 1)

            def front_exp(b):
                act.wait_ge(rt_step, RT_STEPS * b + 3)
                nc.scalar.activation(rt[:, 1], rt[:, 0], ACT.Exp).then_inc(ex_ready, 1)

            front_zT(0, 0)
            front_rh(0, 0)

            def body(b, s):
                gelu(b, s, 0)
                front_exp(b)
                gelu(b, s, 1)
                if not last(b):
                    front_zT(b + 1, 1 - s)
                gelu(b, s, 2)
                if not last(b):
                    front_rh(b + 1, 1 - s)
                gelu(b, s, 3)

            each_batch(act, body)

        @block.vector
        def _(dve):
            nc.vector.memset(r2[:], 0.0).then_inc(r2_zeroed, 1)
            for n, (_, hi, lo) in enumerate(pieces):
                dve.wait_ge(stage_loaded[n % 2], 16 * (n // 2 + 1))
                nc.vector.tensor_copy(hi, staged(n)).then_inc(split_hi, 1)
                dve.wait_ge(split_hi, n + 1)
                nc.vector.tensor_tensor(out=lo, in0=staged(n), in1=hi, op=ALU.subtract).then_inc(split_lo, 1)
            dve.wait_ge(small_loaded, 16 * 7)

            def layernorm(b, s):
                dve.wait_ge(x_loaded[s], 16 * (half(b) + 1))
                k = LN_STEPS * b
                for t in range(T):
                    nc.vector.bn_stats(stats[:, t], x[:, s, t]).then_inc(stats_step, 1)
                wait(dve, zn_ready, T * b)
                for t in range(T):
                    wait_apart(dve, stats_step, k + T, passed)
                    nc.vector.bn_aggr(mv[:, t], stats[:, t]).then_inc(stats_step, 1)
                dve.wait_ge(rstd_ready, b + 1)
                wait(dve, zT_done, b)
                for t in range(T):
                    nc.vector.tensor_scalar(zn[:, t], x[:, s, t], mv[:, t, 0:1], rstd[:, t:t + 1], ALU.subtract,
                                            ALU.mult).then_inc(zn_ready, 1)

            def front_zT(b, s):
                dve.wait_ge(zTh_ready, b + 1)
                nc.vector.tensor_tensor(out=zTl[:, s], in0=pF[:, 0].rearrange("p (k t) -> p k t", k=KC),
                                        in1=zTh[:, s], op=ALU.subtract).then_inc(zTl_ready, 1)

            def front_logits(b):
                dve.wait_ge(lgT_done, b + 1)
                wait(dve, lg_done, b)
                nc.vector.tensor_copy(lgT[:], pF[:, 1, 0:S]).then_inc(lgT_ready, 1)

            def link(b, k, ins):
                ins.then_inc(rt_step, 1)
                dve.wait_ge(rt_step, RT_STEPS * b + k)

            def wide(a):
                return a[:, :, None].broadcast_to([P, T, E])

            def route_logits(b):
                dve.wait_ge(lg_done, b + 1)
                rows = pF[:, 0, 0:T * P].rearrange("p (t k r) -> p t r k", t=T, k=KR)[:, :, 0:E, :]
                nc.vector.tensor_reduce(out=lg[:], in_=rows, axis=AX.X, op=ALU.add).then_inc(lg_ready, 1)
                dve.wait_ge(lg_ready, b + 1)
                link(b, 1, nc.vector.tensor_tensor(out=lg[:], in0=lg[:],
                                                   in1=rb2s[:, None, :].broadcast_to([P, T, E]), op=ALU.add))
                link(b, 2, nc.vector.tensor_reduce(out=rs[:, 0], in_=lg[:], axis=AX.X, op=ALU.max))
                link(b, 3, nc.vector.tensor_tensor(out=rt[:, 0], in0=lg[:], in1=wide(rs[:, 0]), op=ALU.subtract))

            def route_gates(b, s):
                dve.wait_ge(ex_ready, b + 1)
                link(b, 4, nc.vector.tensor_reduce(out=rs[:, 1], in_=rt[:, 1], axis=AX.X, op=ALU.add))
                link(b, 5, nc.vector.reciprocal(rs[:, 2], rs[:, 1]))
                link(b, 6, nc.vector.tensor_tensor(out=rt[:, 2], in0=rt[:, 1], in1=wide(rs[:, 2]), op=ALU.mult))
                mine = rt[:, 2, :, :, None].broadcast_to([P, T, E, E])
                other = rt[:, 2, :, None, :].broadcast_to([P, T, E, E])
                link(b, 7, nc.vector.tensor_tensor(out=cmpg[:], in0=other, in1=mine, op=ALU.is_gt))
                link(b, 8, nc.vector.tensor_tensor(out=cmpe[:], in0=other, in1=mine, op=ALU.is_equal))
                link(b, 9, nc.vector.tensor_tensor(out=cmpe[:], in0=cmpe[:],
                                                   in1=tri[:, None].broadcast_to([P, T, E, E]), op=ALU.mult))
                link(b, 10, nc.vector.tensor_tensor(out=cmpg[:], in0=cmpg[:], in1=cmpe[:], op=ALU.add))
                link(b, 11, nc.vector.tensor_reduce(out=rt[:, 3], in_=cmpg[:], axis=AX.X, op=ALU.add))
                wait(dve, stored[s], 16 * half(b))
                nc.vector.scalar_tensor_tensor(out=gate[:, s], in0=rt[:, 3], scalar=1.5, in1=rt[:, 2],
                                               op0=ALU.is_lt, op1=ALU.mult).then_inc(gate_ready, 1)
                dve.wait_ge(gate_ready, b + 1)
                for e in range(E):
                    for t in range(T):
                        if e:
                            dve.wait_ge(acc_step[t], ACC_STEPS * b + e)
                        nc.vector.scalar_tensor_tensor(
                            out=acc[:, s, t], in0=b2s[:, e], scalar=gate[:, s, t, e:e + 1],
                            in1=acc[:, s, t] if e else x[:, s, t], op0=ALU.mult, op1=ALU.add,
                        ).then_inc(acc_step[t], 1)

            def split_hidden(b, e):
                for u in range(U):
                    n = U * E * b + U * e + u
                    dve.wait_ge(h_ready, 2 * n + 2)
                    wait(dve, y_done, T * (E * b + e - 1))
                    nc.vector.tensor_copy(hh[:, e % 2, 2 * u:2 * u + 2], h[:, u % 2]).then_inc(hh_ready, 1)
                    dve.wait_ge(hh_ready, n + 1)
                    nc.vector.tensor_tensor(out=hl[:, e % 2, 2 * u:2 * u + 2], in0=h[:, u % 2],
                                            in1=hh[:, e % 2, 2 * u:2 * u + 2],
                                            op=ALU.subtract).then_inc(hl_ready, 1)

            def combine(b, s, e):
                for t in range(T):
                    dve.wait_ge(y_done, T * (E * b + e) + t + 1)
                    dve.wait_ge(acc_step[t], ACC_STEPS * b + E + e)
                    nc.vector.scalar_tensor_tensor(out=acc[:, s, t], in0=pY[:, t, 0:C],
                                                   scalar=gate[:, s, t, e:e + 1], in1=acc[:, s, t],
                                                   op0=ALU.mult, op1=ALU.add).then_inc(acc_step[t], 1)

            layernorm(0, 0)
            front_zT(0, 0)
            front_logits(0)
            route_logits(0)

            def body(b, s):
                split_hidden(b, 0)
                if not first(b):
                    combine(b - 1, 1 - s, 3)
                route_gates(b, s)
                if not last(b):
                    layernorm(b + 1, 1 - s)
                split_hidden(b, 1)
                if not last(b):
                    front_zT(b + 1, 1 - s)
                combine(b, s, 0)
                split_hidden(b, 2)
                combine(b, s, 1)
                split_hidden(b, 3)
                if not last(b):
                    front_logits(b + 1)
                combine(b, s, 2)
                if not last(b):
                    route_logits(b + 1)

            each_batch(dve, body)
            combine(B - 1, 1, 3)

        @block.gpsimd
        def _(pool):
            nc.gpsimd.memset(half_power[:], -0.5).then_inc(power_set, 1)
            nc.gpsimd.memset(eps[:], LN_EPS).then_inc(power_set, 1)
            pool.wait_ge(power_set, 2)

            def body(b, s):
                pool.wait_ge(stats_step, LN_STEPS * (b + 1))
                wait(pool, zn_ready, T * b)
                nc.gpsimd.tensor_tensor(out=vare[:], in0=mv[:, :, 1], in1=eps[:], op=ALU.add).then_inc(vare_ready, 1)
                pool.wait_ge(vare_ready, b + 1)
                nc.gpsimd.tensor_tensor(out=rstd[:], in0=vare[:], in1=half_power[:], op=ALU.pow).then_inc(rstd_ready, 1)

            each_batch(pool, body)

        @block.tensor
        def _(pe):
            def product(out_ap, terms):
                for i, (lhsT, rhs) in enumerate(terms):
                    ins = nc.tensor.matmul(out_ap, lhsT, rhs, start=(i == 0), stop=(i == len(terms) - 1))
                return ins

            def front_zT(b, s):
                pe.wait_ge(zn_ready, T * (b + 1))
                wait(pe, lg_ready, b)
                for t in range(T):
                    for k in range(KC):
                        ins = nc.tensor.transpose(pF[:, 0, k * S + t * P:k * S + (t + 1) * P],
                                                  zn[:, t, k * P:(k + 1) * P], ident[:])
                ins.then_inc(zT_done, 1)

            def front_router(b, s):
                pe.wait_ge(zTl_ready, b + 1)
                wait(pe, lgT_ready, b)
                for r in range(KR):
                    cols = slice(r * P, (r + 1) * P)
                    ins = product(pF[:, (r // 2 + 1) % 2, (r % 2) * S:(r % 2 + 1) * S],
                                  [(w[:, k, cols], z[:, s, k]) for k in range(KC)
                                   for w, z in ((r1h, zTh), (r1l, zTh), (r1h, zTl))])
                    if r % 2:
                        ins.then_inc(rh_done, 1)

            def front_logits(b):
                pe.wait_ge(rh_ready, KR * (b + 1))
                for k in range(KR):
                    ins = nc.tensor.matmul(pF[32 * k:32 * k + 32, 1, 0:S], r2[:, k, :], rh[:, k], start=True,
                                           stop=True)
                ins.then_inc(lgT_done, 1)

            def front_logits_back(b):
                pe.wait_ge(lgT_ready, b + 1)
                for t in range(T):
                    ins = nc.tensor.transpose(pF[:, 0, t * P:(t + 1) * P], lgT[:, t * P:(t + 1) * P], ident[:])
                ins.then_inc(lg_done, 1)

            def hidden(b, s, e):
                pe.wait_ge(zTl_ready, b + 1)
                for u in range(U):
                    wait(pe, h_ready, 2 * (U * E * b + U * (e - 1) + u) + 2)
                    for j in range(2):
                        cols = slice((2 * u + j) * P, (2 * u + j + 1) * P)
                        ins = product(pH[:, u, j * S:(j + 1) * S],
                                      [(w[:, e, k, cols], z[:, s, k]) for k in range(KC)
                                       for w, z in ((w1h, zTh), (w1l, zTh), (w1h, zTl))])
                    ins.then_inc(hid_done, 1)

            def down(b, e):
                pe.wait_ge(hl_ready, U * (E * b + e + 1))
                for t in range(T):
                    n = E * b + e
                    wait(pe, acc_step[t], ACC_STEPS * b + E + e if e else ACC_STEPS * b)
                    rows = slice(t * P, (t + 1) * P)
                    product(pY[:, t, 0:C],
                            [(a[:, e % 2, k, rows], w[:, e, k]) for k in range(KH)
                             for a, w in ((hh, w2h), (hh, w2l), (hl, w2h))]).then_inc(y_done, 1)

            pe.wait_ge(small_loaded, 16 * 7)
            pe.wait_ge(split_lo, len(pieces))
            front_zT(0, 0)
            front_router(0, 0)
            front_logits(0)
            front_logits_back(0)

            def body(b, s):
                hidden(b, s, 0)
                if not first(b):
                    down(b - 1, 3)
                hidden(b, s, 1)
                if not last(b):
                    front_zT(b + 1, 1 - s)
                down(b, 0)
                hidden(b, s, 2)
                if not last(b):
                    front_router(b + 1, 1 - s)
                down(b, 1)
                hidden(b, s, 3)
                if not last(b):
                    front_logits(b + 1)
                down(b, 2)
                if not last(b):
                    front_logits_back(b + 1)

            each_batch(pe, body)
            down(B - 1, 3)


def build_layer(nc, a, out):
    B, S, C = a["x"].shape
    x2 = nc.dram_tensor("x2_scratch", (B, S, C), F32, kind="Internal").ap()
    qk = nc.dram_tensor("qk_scratch", (B, 4, C, S), F32, kind="Internal").ap()
    build_attention(nc, a["x"], a["ctx"], a["mask"], a["ident"], a["blocks"], a["heads"], a["wqkvT"], a["woutT"],
                    a["b_out"], a["wqT"], a["bq"], a["wkT"], a["bk"], a["wvT"], a["bv"], a["woT"], a["bo"], qk, x2)
    build_moe(nc, x2, a["ident"], a["before"], a["rW1"], a["rb1"], a["rW2"], a["rb2"], a["We1"], a["be1"],
              a["We2"], a["be2"], out)


def kernel(**inputs):
    import numpy as np
    import concourse.bacc as bacc
    from concourse.bass_utils import run_bass_kernel_spmd

    f = {k: np.asarray(v) for k, v in inputs.items()}
    C, D = f["x"].shape[2], f["x"].shape[2] // HEADS
    E, HID = f["L0_ffn_be1"].shape
    block = np.kron(np.eye(P // D), np.full((D, D), D ** -0.5)).astype(np.float32)
    arrays = {
        "x": f["x"], "ctx": f["ctx_1024"], "mask": f["mask_BxSxS2_ff0"],
        "ident": np.eye(P, dtype=np.float32),
        "blocks": block, "heads": np.ascontiguousarray(block[:, ::D]),
        "before": np.broadcast_to(np.tril(np.ones((E, E), np.float32), -1), (P, E, E)),
        "wqkvT": f["L0_attn_w_qkv"].T, "woutT": f["L0_attn_w_out"].T, "b_out": f["L0_attn_b_out"],
        "wqT": f["L0_xattn_Wq"].T, "bq": f["L0_xattn_bq"].reshape(-1, P).T,
        "wkT": f["L0_xattn_Wk"].T, "bk": f["L0_xattn_bk"].reshape(-1, P).T,
        "wvT": f["L0_xattn_Wv"].T, "bv": f["L0_xattn_bv"],
        "woT": f["L0_xattn_Wo"].T, "bo": f["L0_xattn_bo"],
        "rW1": f["L0_ffn_rW1"], "rb1": f["L0_ffn_rb1"].reshape(-1, P).T, "rW2": f["L0_ffn_rW2"],
        "rb2": f["L0_ffn_rb2"], "We1": f["L0_ffn_We1"],
        "be1": f["L0_ffn_be1"].reshape(E, -1, P).transpose(2, 0, 1), "We2": f["L0_ffn_We2"],
        "be2": f["L0_ffn_be2"],
    }
    arrays = {k: np.ascontiguousarray(v) for k, v in arrays.items()}
    nc = bacc.Bacc("TRN2", target_bir_lowering=False, num_devices=1)
    a = {k: nc.dram_tensor(k, v.shape, mybir.dt.from_np(v.dtype), kind="ExternalInput").ap()
         for k, v in arrays.items()}
    out = nc.dram_tensor("out", f["x"].shape, F32, kind="ExternalOutput").ap()
    build_layer(nc, a, out)
    r = run_bass_kernel_spmd(nc, [arrays], core_ids=[0])
    return r.results[0]["out"]
```

```python
from contextlib import ExitStack

import concourse.bass as bass
from concourse import mybir

P = 128
F32 = mybir.dt.float32
F32R = mybir.dt.float32r
I32 = mybir.dt.int32
ALU = mybir.AluOpType
ACT = mybir.ActivationFunctionType
AX = mybir.AxisListType
LN_EPS = 1e-5
DEN_EPS = 1e-6
HEADS = 16
BIG = 3.0e38


def wait(engine, semaphore, value):
    if not isinstance(value, int) or value > 0:
        engine.wait_ge(semaphore, value)


def wait_apart(engine, semaphore, value, passed):
    wait(engine, semaphore, value)
    engine.sem_inc(passed, 1)


def build_attention(nc, x, ctx_in, mask, ident_in, block_in, heads_in, wqkvT, woutT, b_out, wqT, bq, wkT, bk, wvT, bv,
                    woT, bo, qk_dram, x2):
    B, S, C = x.shape
    H = HEADS
    D = C // H
    T = S // P
    KC = C // P
    SCALE = D ** -0.5
    HB = P // D
    HP = H // 2
    G = H // 4
    W1 = P + HB
    with ExitStack() as ctx:
        def sb(name, shape, dt=F32):
            return ctx.enter_context(nc.sbuf_tensor("a_" + name, shape, dt))

        def sem(name):
            return ctx.enter_context(nc.semaphore("a_" + name))

        def pair(name, shape):
            return sb(name + "h", shape, F32R), sb(name + "l", shape, F32R)

        NW = 8
        LQ, LK, LV, LO, CQ, CK, CV, CO = range(NW)
        wh, wl = pair("w", [P, NW, KC, C])
        stage = sb("stage", [P, 2, KC, C])
        ident = sb("ident", [P, P])
        blocks = sb("blocks", [P, P])
        heads = sb("heads", [P, HB])
        boutb = sb("boutb", [P, C])
        bvb = sb("bvb", [P, C])
        bob = sb("bob", [P, C])
        bqk = sb("bqk", [P, 2, KC])
        half_power = sb("half_power", [P, T])
        eps = sb("eps", [P, T])

        xs = sb("x", [P, T, C])
        xb = sb("xb", [P, T, C])
        stats = sb("stats", [P, 2, T, 6])
        mv = sb("mv", [P, 2, T, 2])
        vare = sb("vare", [P, 2, T])
        rstd = sb("rstd", [P, 2, T])
        zn = sb("zn", [P, 2, T, C])
        xTh, xTl = pair("xT", [P, KC, S])
        qm = sb("qm", [P, 2, 2 * C])
        qe = sb("qe", [P, 2, 2 * C])
        q1T = sb("q1T", [P, KC, S])
        k1 = sb("k1", [P, T, C])
        v1 = sb("v1", [P, T, KC, P + 1])
        kvm = sb("kvm", [P, KC, W1])
        den = sb("den", [P, T, KC, HB])
        rden = sb("rden", [P, T, KC, HB])
        o1 = sb("o1", [P, T, C])
        oTh, oTl = pair("oT", [P, KC, S])
        x1 = sb("x1", [P, 2, T, C])
        xr = sb("xr", [P, 2, T, C])
        yTh, yTl = pair("yT", [P, KC, S])
        cs = sb("c", [P, T, C])
        cTh, cTl = pair("cT", [P, KC, S])
        qkf = sb("qkf", [P, 2, KC, S])
        qk = sb("qk", [P, 4, KC, S], F32R)
        vx = sb("vx", [P, 2, T, H, 32])
        ms = sb("mask", [P, 2, T, S])
        Q = sb("Q", [P, H, S], F32R)
        K = sb("K", [P, H, S], F32R)
        sc = sb("sc", [P, 4, T, 2, S])
        nmx = sb("nmx", [P, 4, T, 2])
        PT = sb("PT", [P, 8, 2 * S])
        oS = sb("oS", [P, G, S])
        rd = sb("rd", [P, T, H])
        oN = sb("oN", [P, T, C])
        nTh, nTl = pair("nT", [P, KC, S])
        x2s = sb("x2", [P, T, C])

        pA = ctx.enter_context(nc.psum_tensor("a_pA", [P, 3, 512], F32))
        pS = ctx.enter_context(nc.psum_tensor("a_pS", [P, T, 2, S], F32))
        pP = ctx.enter_context(nc.psum_tensor("a_pP", [P, 2, 512], F32))
        pO = ctx.enter_context(nc.psum_tensor("a_pO", [P, 512], F32))

        ident_loaded, small_loaded = sem("ident_loaded"), sem("small_loaded")
        passed = sem("passed")
        stage_loaded = [sem(f"stage_loaded{i}") for i in range(2)]
        split_hi, split_lo = sem("split_hi"), sem("split_lo")
        pool_set, dve_set, act_set = sem("pool_set"), sem("dve_set"), sem("act_set")
        x_loaded, c_loaded = sem("x_loaded"), sem("c_loaded")
        m_loaded = [sem(f"m_loaded{i}") for i in range(2)]
        stats_step = [sem(f"stats_step{i}") for i in range(2)]
        vare_ready = [sem(f"vare_ready{i}") for i in range(2)]
        rstd_ready = [sem(f"rstd_ready{i}") for i in range(2)]
        zn_ready = [sem(f"zn_ready{i}") for i in range(2)]
        xb_ready, xr_ready = sem("xb_ready"), sem("xr_ready")
        xT_done, xTh_ready, xTl_ready = sem("xT_done"), sem("xTh_ready"), sem("xTl_ready")
        lq_done, lk_done, lv_done = sem("lq_done"), sem("lk_done"), sem("lv_done")
        qm_ready, km_ready = sem("qm_ready"), sem("km_ready")
        qe_ready, ke_ready = sem("qe_ready"), sem("ke_ready")
        q1_ready, k1_ready, v1_ready = sem("q1_ready"), sem("k1_ready"), sem("v1_ready")
        kv_done, kvm_ready = sem("kv_done"), sem("kvm_ready")
        o1_done, den_ready, rden_ready, o1_ready = sem("o1_done"), sem("den_ready"), sem("rden_ready"), sem("o1_ready")
        oT_done, oTh_ready, oTl_ready = sem("oT_done"), sem("oTh_ready"), sem("oTl_ready")
        x1_done, x1_ready = sem("x1_done"), sem("x1_ready")
        yT_done, yTh_ready, yTl_ready = sem("yT_done"), sem("yTh_ready"), sem("yTl_ready")
        cT_done, cTh_ready, cTl_ready = sem("cT_done"), sem("cTh_ready"), sem("cTl_ready")
        cq_done, ck_done, cv_done = sem("cq_done"), sem("ck_done"), sem("cv_done")
        qf_ready, kf_ready = sem("qf_ready"), sem("kf_ready")
        qh_ready, ql_ready, kh_ready, kl_ready = sem("qh_ready"), sem("ql_ready"), sem("kh_ready"), sem("kl_ready")
        vx_ready = sem("vx_ready")
        qk_stored = sem("qk_stored")
        qk_loaded = [sem(f"qk_loaded{i}") for i in range(KC)]
        s_done, s_ready, p_ready = sem("s_done"), sem("s_ready"), sem("p_ready")
        pT_done = sem("pT_done")
        pT_ready = [sem(f"pT_ready{i}") for i in range(2)]
        pv_done, oS_ready = sem("pv_done"), sem("oS_ready")
        nq_done, rd_ready, oN_ready = sem("nq_done"), sem("rd_ready"), sem("oN_ready")
        nT_done, nTh_ready, nTl_ready = sem("nT_done"), sem("nTh_ready"), sem("nTl_ready")
        x2_done, x2_ready, x2_stored = sem("x2_done"), sem("x2_ready"), sem("x2_stored")

        BANK = {name: i % 3 for i, name in enumerate(
            ("cT", "yT", "xT", "n0", "n1", "cq", "lk", "ck", "lq", "lv", "kv", "nT",
             "x2", "cv", "o0", "o1", "oT", "x1"))}
        READER = {
            "cT": (cTl_ready, lambda b: b + 1), "xT": (xTl_ready, lambda b: b + 1),
            "yT": (yTl_ready, lambda b: b + 1), "n0": (oN_ready, lambda b: T * b + 1),
            "n1": (oN_ready, lambda b: T * b + 2), "lq": (q1_ready, lambda b: b + 1),
            "lk": (k1_ready, lambda b: b + 1), "cq": (qf_ready, lambda b: KC * (b + 1)),
            "lv": (v1_ready, lambda b: b + 1), "nT": (nTl_ready, lambda b: b + 1),
            "ck": (kf_ready, lambda b: KC * (b + 1)), "kv": (kvm_ready, lambda b: 2 * (b + 1)),
            "x2": (x2_ready, lambda b: b + 1), "cv": (vx_ready, lambda b: b + 1),
            "o0": (o1_ready, lambda b: T * b + 1), "o1": (o1_ready, lambda b: T * b + 2),
            "oT": (oTl_ready, lambda b: b + 1), "x1": (x1_ready, lambda b: b + 1),
        }

        def each_batch(engine, body):
            body(0, 0)
            body(1, 1)
            with engine.Fori(1, B // 2 - 1) as i:
                body(i * 2, 0)
                body(i * 2 + 1, 1)
            body(B - 2, 0)
            body(B - 1, 1)

        def has(b):
            return not isinstance(b, int) or 0 <= b < B

        def rows(dram, b):
            v = dram.rearrange("b (t p) c -> b p t c", p=P)
            return v[b] if isinstance(b, int) else v[bass.ds(b, 1)].rearrange("o p t c -> (o p) t c")

        def bank(name):
            return pA[:, BANK[name], :]

        def halves(name):
            return bank(name).rearrange("p (k t) -> p k t", k=2)

        def heads_of(name):
            return bank(name)[:, 0:KC * W1].rearrange("p (m w) -> p m w", m=KC)

        block = ctx.enter_context(nc.Block())

        @block.sync
        def _(sp):
            def load_x(b):
                wait_apart(sp, zn_ready[0], T * b, passed)
                wait_apart(sp, xb_ready, b, passed)
                sp.dma_start(xs[:], rows(x, b)).then_inc(x_loaded, 16)

            def load_c(b):
                wait_apart(sp, cT_done, b, passed)
                sp.dma_start(cs[:], rows(ctx_in, b)).then_inc(c_loaded, 16)

            def load_mask(b, s):
                wait_apart(sp, s_ready, 2 * H * (b - 1), passed)
                sp.dma_start(ms[:, s], rows(mask, b)).then_inc(m_loaded[s], 16)

            def scratch(b):
                v = qk_dram.rearrange("b f (m p) t -> b p f m t", p=P)
                return v[b] if isinstance(b, int) else v[bass.ds(b, 1)].rearrange("o p f m t -> (o p) f m t")

            def spread(b, part, m):
                v = qk_dram.rearrange("b f (m h d) t -> b f m d h t", m=KC, d=D)
                if isinstance(b, int):
                    return v[b, part, m]
                return v[bass.ds(b, 1), part, m].rearrange("o d h t -> (o d) h t")

            def store_qk(b):
                wait_apart(sp, ql_ready, b + 1, passed)
                wait_apart(sp, kl_ready, b + 1, passed)
                sp.dma_start(scratch(b), qk[:].bitcast(F32)).then_inc(qk_stored, 16)

            def load_qk(b, m):
                wait_apart(sp, qk_stored, 16 * (b + 1), passed)
                wait_apart(sp, s_done, 2 * HP * (b - 1) + HP * (m + 1), passed)
                for tile, parts in ((Q, (0, 1, 0)), (K, (2, 2, 3))):
                    for i, part in enumerate(parts):
                        sp.dma_start(tile[D * i:D * (i + 1), m * HB:(m + 1) * HB, :].bitcast(F32),
                                     spread(b, part, m)).then_inc(qk_loaded[m], 16)

            def store_x2(b):
                wait_apart(sp, x2_ready, b + 1, passed)
                sp.dma_start(rows(x2, b), x2s[:]).then_inc(x2_stored, 16)

            load_x(0)
            sp.dma_start(ident[:], ident_in).then_inc(ident_loaded, 16)
            wT = [wqkvT[:, 0:C], wqkvT[:, C:2 * C], wqkvT[:, 2 * C:3 * C], woutT, wqT, wkT, wvT, woT]

            def load_weight(n):
                wait_apart(sp, split_lo, n - 1, passed)
                sp.dma_start(stage[:, n % 2],
                             wT[n].rearrange("(k p) n -> p k n", p=P)).then_inc(stage_loaded[n % 2], 16)

            load_weight(LQ)
            load_weight(LK)
            for dst, src in ((blocks[:], block_in), (heads[:], heads_in),
                             (boutb[:], b_out[None, :].broadcast_to([P, C])),
                             (bvb[:], bv[None, :].broadcast_to([P, C])), (bob[:], bo[None, :].broadcast_to([P, C])),
                             (bqk[:, 0], bq), (bqk[:, 1], bk)):
                sp.dma_start(dst, src).then_inc(small_loaded, 16)
            load_weight(LV)
            load_weight(LO)
            load_c(0)
            load_x(1)
            for n in (CQ, CK, CV, CO):
                load_weight(n)
            load_mask(0, 0)
            load_mask(1, 1)
            load_c(1)
            sp.wait_ge(pool_set, 4)
            store_qk(0)
            load_qk(0, 0)
            load_qk(0, 1)

            def body(b, s):
                if s == 0 and has(b + 2):
                    load_x(b + 2)
                if has(b + 2):
                    load_c(b + 2)
                if s == 0 and has(b + 3):
                    load_x(b + 3)
                if has(b + 1):
                    store_qk(b + 1)
                    load_qk(b + 1, 0)
                if has(b - 1):
                    store_x2(b - 1)
                if has(b + 1):
                    load_qk(b + 1, 1)
                if has(b + 2):
                    load_mask(b + 2, s)

            each_batch(sp, body)
            store_x2(B - 1)
            sp.wait_ge(x2_stored, 16 * B)

        @block.gpsimd
        def _(pool):
            nc.gpsimd.memset(half_power[:], -0.5).then_inc(pool_set, 1)
            nc.gpsimd.memset(eps[:], LN_EPS).then_inc(pool_set, 1)
            pool.wait_ge(pool_set, 2)

            def rsqrt(b, i):
                pool.wait_ge(stats_step[i], 2 * T * (b + 1))
                wait(pool, zn_ready[i], T * b)
                nc.gpsimd.tensor_tensor(out=vare[:, i], in0=mv[:, i, :, 1], in1=eps[:],
                                        op=ALU.add).then_inc(vare_ready[i], 1)
                pool.wait_ge(vare_ready[i], b + 1)
                nc.gpsimd.tensor_tensor(out=rstd[:, i], in0=vare[:, i], in1=half_power[:],
                                        op=ALU.pow).then_inc(rstd_ready[i], 1)

            def add_bout(b):
                pool.wait_ge(x_loaded, 16 * (b + 1))
                wait(pool, x1_ready, b)
                nc.gpsimd.tensor_tensor(out=xb[:], in0=xs[:], in1=boutb[:, None, :].broadcast_to([P, T, C]),
                                        op=ALU.add).then_inc(xb_ready, 1)

            def add_bo(b, s):
                pool.wait_ge(x1_ready, b + 1)
                wait(pool, x2_ready, b - 1)
                nc.gpsimd.tensor_tensor(out=xr[:, s], in0=x1[:, s], in1=bob[:, None, :].broadcast_to([P, T, C]),
                                        op=ALU.add).then_inc(xr_ready, 1)

            rsqrt(0, 0)
            pool.wait_ge(small_loaded, 16 * 7)
            add_bout(0)
            nc.gpsimd.memset(Q[:].bitcast(F32), 0.0).then_inc(pool_set, 1)
            nc.gpsimd.memset(K[:].bitcast(F32), 0.0).then_inc(pool_set, 1)
            rsqrt(0, 1)
            add_bo(0, 0)
            rsqrt(1, 0)
            add_bout(1)

            def body(b, s):
                if has(b + 1):
                    rsqrt(b + 1, 1)
                if has(b + 2):
                    rsqrt(b + 2, 0)
                if has(b + 2):
                    add_bout(b + 2)
                if has(b + 1):
                    add_bo(b + 1, 1 - s)

            each_batch(pool, body)

        @block.scalar
        def _(act):
            act.wait_ge(small_loaded, 16 * 7)

            def high_part(done, ready, name, out, b, reader):
                act.wait_ge(done, b + 1)
                for used, n in reader:
                    wait(act, used, n)
                nc.scalar.copy(out[:], halves(name)).then_inc(ready, 1)

            def x_high(b):
                high_part(xT_done, xTh_ready, "xT", xTh, b, [(lv_done, b)])

            def exp_q(b):
                act.wait_ge(qm_ready, b + 1)
                wait(act, q1_ready, b)
                nc.scalar.activation(qe[:, 0], qm[:, 0], ACT.Exp).then_inc(qe_ready, 1)

            def exp_k(b):
                act.wait_ge(km_ready, b + 1)
                wait(act, k1_ready, b)
                nc.scalar.activation(qe[:, 1], qm[:, 1], ACT.Exp).then_inc(ke_ready, 1)

            def copy_v1(b):
                act.wait_ge(lv_done, b + 1)
                wait(act, kv_done, b)
                nc.scalar.copy(v1[:, :, :, 0:P],
                               bank("lv").rearrange("p (t m c) -> p t m c", t=T, m=KC)).then_inc(v1_ready, 1)

            def o_high(b):
                high_part(oT_done, oTh_ready, "oT", oTh, b, [(x1_done, b)])

            def y_high(b):
                high_part(yT_done, yTh_ready, "yT", yTh, b, [(cq_done, b)])

            def c_high(b):
                high_part(cT_done, cTh_ready, "cT", cTh, b, [(cv_done, b)])

            def n_high(b):
                high_part(nT_done, nTh_ready, "nT", nTh, b, [(x2_done, b)])

            def biased(b, i, name, done, ready, low_ready, scale):
                act.wait_ge(done, b + 1)
                wait(act, low_ready, b)
                for m in range(KC):
                    nc.scalar.activation(qkf[:, i, m], halves(name)[:, m], ACT.Identity, bias=bqk[:, i, m:m + 1],
                                         scale=scale).then_inc(ready, 1)

            def cross_q(b):
                biased(b, 0, "cq", cq_done, qf_ready, ql_ready, SCALE)

            def cross_k(b):
                biased(b, 1, "ck", ck_done, kf_ready, kl_ready, 1.0)

            def exps(b, hp):
                for t in range(T):
                    for j in range(2):
                        act.wait_ge(s_ready, 2 * H * b + 4 * hp + 2 * t + j + 1)
                        nc.scalar.activation(sc[:, hp % 4, t, j], sc[:, hp % 4, t, j], ACT.Exp,
                                             bias=nmx[:, hp % 4, t, j:j + 1], scale=-1.0).then_inc(p_ready, 1)

            def take_pT(b, hp):
                h = 2 * hp
                act.wait_ge(pT_done, H * b + h + 1)
                wait(act, pv_done, G * b + h // 4 - 1)
                nc.scalar.copy(PT[:, h % 8], pP[:, 0]).then_inc(pT_ready[0], 1)

            def take_pT_odd(b, hp):
                h = 2 * hp + 1
                act.wait_ge(pT_done, H * b + h + 1)
                wait(act, pv_done, G * b + h // 4 - 1)
                nc.scalar.copy(PT[:, h % 8], pP[:, 1]).then_inc(pT_ready[1], 1)

            def take_pO(b, g):
                act.wait_ge(pv_done, G * b + g + 1)
                wait(act, nq_done, T * b)
                nc.scalar.copy(oS[:, g], pO[:, 0:S]).then_inc(oS_ready, 1)

            nc.scalar.mul(bqk[:, 0], bqk[:, 0], SCALE).then_inc(act_set, 1)
            act.wait_ge(act_set, 1)
            def linear(b):
                x_high(b)
                exp_k(b)
                exp_q(b)
                copy_v1(b)
                o_high(b)

            linear(0)
            c_high(0)
            y_high(0)
            cross_k(0)
            cross_q(0)
            linear(1)

            def body(b, s):
                A, V, F = b + 2, b + 1, b - 1
                exps(b, 0)
                if has(V):
                    c_high(V)
                if has(F):
                    take_pT(F, 7)
                exps(b, 1)
                if has(F):
                    take_pO(F, 3)
                take_pT(b, 0)
                if has(A):
                    x_high(A)
                if has(V):
                    y_high(V)
                exps(b, 2)
                take_pT(b, 1)
                take_pT_odd(b, 1)
                take_pT(b, 2)
                if has(V):
                    cross_q(V)
                if has(A):
                    exp_k(A)
                if has(V):
                    cross_k(V)
                exps(b, 3)
                take_pO(b, 0)
                if has(A):
                    exp_q(A)
                    copy_v1(A)
                exps(b, 4)
                take_pT(b, 3)
                if has(F):
                    n_high(F)
                exps(b, 5)
                exps(b, 6)
                take_pT(b, 4)
                take_pT_odd(b, 4)
                if has(A):
                    o_high(A)
                take_pT(b, 5)
                take_pO(b, 1)
                exps(b, 7)
                take_pT(b, 6)
                take_pT_odd(b, 6)
                take_pO(b, 2)

            each_batch(act, body)
            take_pT(B - 1, 7)
            take_pO(B - 1, 3)
            n_high(B - 1)

        @block.vector
        def _(dve):
            nc.vector.memset(v1[:], 1.0).then_inc(dve_set, 1)
            nc.vector.memset(vx[:], 0.0).then_inc(dve_set, 1)
            dve.wait_ge(dve_set, 2)
            nc.vector.memset(vx[:, :, :, :, D:D + 1], 1.0).then_inc(dve_set, 1)

            def split(n):
                dve.wait_ge(stage_loaded[n % 2], 16 * (n // 2 + 1))
                nc.vector.tensor_copy(wh[:, n], stage[:, n % 2]).then_inc(split_hi, 1)
                dve.wait_ge(split_hi, n + 1)
                nc.vector.tensor_tensor(out=wl[:, n], in0=stage[:, n % 2], in1=wh[:, n],
                                        op=ALU.subtract).then_inc(split_lo, 1)

            def moments(b, i, src):
                wait(dve, zn_ready[i], T * b)
                for t in range(T):
                    nc.vector.bn_stats(stats[:, i, t], src[:, t]).then_inc(stats_step[i], 1)
                wait_apart(dve, stats_step[i], 2 * T * b + T, passed)
                for t in range(T):
                    nc.vector.bn_aggr(mv[:, i, t], stats[:, i, t]).then_inc(stats_step[i], 1)

            def layernorm(b, i, src, transposed):
                dve.wait_ge(rstd_ready[i], b + 1)
                wait(dve, transposed, b)
                for t in range(T):
                    nc.vector.tensor_scalar(zn[:, i, t], src[:, t], mv[:, i, t, 0:1], rstd[:, i, t:t + 1],
                                            ALU.subtract, ALU.mult).then_inc(zn_ready[i], 1)

            def moments_x(b):
                dve.wait_ge(x_loaded, 16 * (b + 1))
                moments(b, 0, xs)

            def norm_x(b):
                layernorm(b, 0, xs, xT_done)

            def moments_x1(b, s):
                dve.wait_ge(x1_ready, b + 1)
                moments(b, 1, x1[:, s])

            def norm_x1(b, s):
                layernorm(b, 1, x1[:, s], yT_done)

            def low_part(high_ready, ready, name, high, low, b):
                dve.wait_ge(high_ready, b + 1)
                nc.vector.tensor_tensor(out=low[:], in0=halves(name), in1=high[:],
                                        op=ALU.subtract).then_inc(ready, 1)

            def x_low(b):
                low_part(xTh_ready, xTl_ready, "xT", xTh, xTl, b)

            def o_low(b):
                low_part(oTh_ready, oTl_ready, "oT", oTh, oTl, b)

            def y_low(b):
                low_part(yTh_ready, yTl_ready, "yT", yTh, yTl, b)

            def c_low(b):
                low_part(cTh_ready, cTl_ready, "cT", cTh, cTl, b)

            def n_low(b):
                low_part(nTh_ready, nTl_ready, "nT", nTh, nTl, b)

            def negative(b, i, name, done, exp_ready, ready):
                dve.wait_ge(done, b + 1)
                wait(dve, exp_ready, b)
                nc.vector.tensor_scalar(qm[:, i], bank(name), 0.0, 1.0, ALU.min, ALU.mult).then_inc(ready, 1)

            def feature(b, i, name, exp_ready, used, out, ready):
                dve.wait_ge(exp_ready, b + 1)
                wait(dve, used, b)
                nc.vector.scalar_tensor_tensor(out=out, in0=bank(name), scalar=0.0, in1=qe[:, i], op0=ALU.max,
                                               op1=ALU.add).then_inc(ready, 1)

            def neg_q(b):
                negative(b, 0, "lq", lq_done, qe_ready, qm_ready)

            def neg_k(b):
                negative(b, 1, "lk", lk_done, ke_ready, km_ready)

            def feat_q(b):
                wait(dve, o1_done, T * b)
                feature(b, 0, "lq", qe_ready, o1_done, q1T[:].rearrange("p k t -> p (k t)"), q1_ready)

            def feat_k(b):
                feature(b, 1, "lk", ke_ready, kv_done, k1[:].rearrange("p t c -> p (t c)"), k1_ready)

            def mask_kv(b):
                dve.wait_ge(kv_done, b + 1)
                wait(dve, o1_done, T * b)
                kv = bank("kv")[:, 0:KC * (P + 1)].rearrange("p (m w) -> p m w", m=KC)
                nc.vector.tensor_tensor(out=kvm[:, :, 0:P], in0=kv[:, :, 0:P],
                                        in1=blocks[:, None, :].broadcast_to([P, KC, P]),
                                        op=ALU.mult).then_inc(kvm_ready, 1)
                nc.vector.tensor_tensor(out=kvm[:, :, P:W1], in0=kv[:, :, P:P + 1].broadcast_to([P, KC, HB]),
                                        in1=heads[:, None, :].broadcast_to([P, KC, HB]),
                                        op=ALU.mult).then_inc(kvm_ready, 1)

            def divide(b):
                for t in range(T):
                    dve.wait_ge(o1_done, T * b + t + 1)
                    nc.vector.tensor_scalar(den[:, t], heads_of(f"o{t}")[:, :, P:W1], DEN_EPS, 1.0, ALU.add,
                                            ALU.mult).then_inc(den_ready, 1)
                wait(dve, o1_ready, T * b)
                dve.wait_ge(den_ready, T * (b + 1))
                nc.vector.reciprocal(rden[:], den[:]).then_inc(rden_ready, 1)
                dve.wait_ge(rden_ready, b + 1)
                wait(dve, oT_done, b)
                for t in range(T):
                    nc.vector.tensor_tensor(
                        out=o1[:, t].rearrange("p (m h d) -> p m h d", m=KC, d=D),
                        in0=heads_of(f"o{t}")[:, :, 0:P].rearrange("p m (h d) -> p m h d", d=D),
                        in1=rden[:, t][:, :, :, None].broadcast_to([P, KC, HB, D]), op=ALU.mult,
                    ).then_inc(o1_ready, 1)

            def residual_1(b, s):
                dve.wait_ge(x1_done, b + 1)
                dve.wait_ge(xb_ready, b + 1)
                wait(dve, xr_ready, b - 1)
                nc.vector.tensor_tensor(out=x1[:, s], in0=bank("x1").rearrange("p (t c) -> p t c", t=T), in1=xb[:],
                                        op=ALU.add).then_inc(x1_ready, 1)

            def split_qk(b, i, float_ready, high_ready, ready):
                dve.wait_ge(float_ready, KC * (b + 1))
                wait(dve, qk_stored, 16 * b)
                nc.vector.tensor_copy(qk[:, 2 * i], qkf[:, i]).then_inc(high_ready, 1)
                dve.wait_ge(high_ready, b + 1)
                nc.vector.tensor_tensor(out=qk[:, 2 * i + 1], in0=qkf[:, i], in1=qk[:, 2 * i],
                                        op=ALU.subtract).then_inc(ready, 1)

            def split_q(b):
                split_qk(b, 0, qf_ready, qh_ready, ql_ready)

            def split_k(b):
                split_qk(b, 1, kf_ready, kh_ready, kl_ready)

            def cross_v(b, s):
                dve.wait_ge(cv_done, b + 1)
                wait(dve, pv_done, G * (b - 1))
                nc.vector.tensor_tensor(out=vx[:, s, :, :, 0:D],
                                        in0=bank("cv").rearrange("p (t h d) -> p t h d", t=T, d=D),
                                        in1=bvb[:].rearrange("p (h d) -> p h d", d=D)[:, None].broadcast_to(
                                            [P, T, H, D]), op=ALU.add).then_inc(vx_ready, 1)

            def scores(b, s, hp):
                if hp == 0:
                    dve.wait_ge(m_loaded[s], 16 * (b // 2 + 1))
                wait(dve, pT_done, H * b + 2 * (hp - 3))
                for t in range(T):
                    wait_apart(dve, s_done, 2 * HP * b + 2 * hp + t + 1, passed)
                    for j in range(2):
                        nc.vector.tensor_tensor_reduce(
                            out=sc[:, hp % 4, t, j], in0=pS[:, t, j], in1=ms[:, s, t], scale=-1.0,
                            scalar=BIG, op0=ALU.add, op1=ALU.min,
                            accum_out=nmx[:, hp % 4, t, j:j + 1]).then_inc(s_ready, 1)

            def take_pT(b, hp):
                h = 2 * hp + 1
                dve.wait_ge(pT_done, H * b + h + 1)
                wait(dve, pv_done, G * b + h // 4 - 1)
                nc.vector.tensor_copy(PT[:, h % 8], pP[:, 1]).then_inc(pT_ready[1], 1)

            def normalise(b):
                for t in range(T):
                    dve.wait_ge(nq_done, T * b + t + 1)
                    o = bank(f"n{t}").rearrange("p (h w) -> p h w", w=32)
                    wait(dve, oN_ready, T * b)
                    nc.vector.reciprocal(rd[:, t], o[:, :, D]).then_inc(rd_ready, 1)
                    dve.wait_ge(rd_ready, T * b + t + 1)
                    wait(dve, nT_done, b)
                    nc.vector.tensor_tensor(out=oN[:, t].rearrange("p (h d) -> p h d", d=D), in0=o[:, :, 0:D],
                                            in1=rd[:, t][:, :, None].broadcast_to([P, H, D]),
                                            op=ALU.mult).then_inc(oN_ready, 1)

            def residual_2(b, s):
                dve.wait_ge(x2_done, b + 1)
                dve.wait_ge(xr_ready, b + 1)
                wait(dve, x2_stored, 16 * b)
                nc.vector.tensor_tensor(out=x2s[:], in0=bank("x2").rearrange("p (t c) -> p t c", t=T),
                                        in1=xr[:, s], op=ALU.add).then_inc(x2_ready, 1)

            def linear(b):
                if b:
                    moments_x(b)
                norm_x(b)
                x_low(b)
                neg_k(b)
                feat_k(b)
                neg_q(b)
                feat_q(b)
                if b == 0:
                    split(LO)
                mask_kv(b)
                divide(b)
                o_low(b)
                if b == 0:
                    split(CQ)
                residual_1(b, b)

            moments_x(0)
            for n in (LQ, LK, LV):
                split(n)
            dve.wait_ge(small_loaded, 16 * 7)
            linear(0)
            moments_x1(0, 0)
            split(CK)
            norm_x1(0, 0)
            c_low(0)
            y_low(0)
            split(CV)
            split_k(0)
            split_q(0)
            cross_v(0, 0)
            linear(1)
            split(CO)
            scores(0, 0, 0)

            def body(b, s):
                A, V, F = b + 2, b + 1, b - 1
                if has(V):
                    moments_x1(V, 1 - s)
                scores(b, s, 1)
                if has(F):
                    take_pT(F, 7)
                if has(A):
                    moments_x(A)
                if has(V):
                    norm_x1(V, 1 - s)
                    c_low(V)
                if has(A):
                    norm_x(A)
                scores(b, s, 2)
                take_pT(b, 0)
                if has(A):
                    x_low(A)
                if has(V):
                    y_low(V)
                scores(b, s, 3)
                if has(F):
                    normalise(F)
                if has(V):
                    split_q(V)
                if has(A):
                    neg_k(A)
                scores(b, s, 4)
                if has(A):
                    feat_k(A)
                    neg_q(A)
                if has(V):
                    split_k(V)
                take_pT(b, 2)
                if has(A):
                    feat_q(A)
                scores(b, s, 5)
                take_pT(b, 3)
                if has(F):
                    n_low(F)
                scores(b, s, 6)
                if has(A):
                    mask_kv(A)
                if has(F):
                    residual_2(F, 1 - s)
                if has(V):
                    cross_v(V, 1 - s)
                if has(A):
                    divide(A)
                scores(b, s, 7)
                take_pT(b, 5)
                if has(A):
                    o_low(A)
                if has(V):
                    scores(V, 1 - s, 0)
                if has(A):
                    residual_1(A, s)

            each_batch(dve, body)
            take_pT(B - 1, 7)
            normalise(B - 1)
            n_low(B - 1)
            residual_2(B - 1, 1)

        @block.tensor
        def _(pe):
            occupant = [None, None, None]

            def take_bank(name, b):
                r = BANK[name]
                if occupant[r] is not None:
                    before, of = occupant[r]
                    semaphore, count = READER[before]
                    pe.wait_ge(semaphore, count(of))
                occupant[r] = (name, b)
                return pA[:, r, :]

            def product(out_ap, terms):
                for i, (lhsT, rhs) in enumerate(terms):
                    ins = nc.tensor.matmul(out_ap, lhsT, rhs, start=(i == 0), stop=(i == len(terms) - 1))
                return ins

            def transposed(name, b, src, done, ready):
                for semaphore, n in ready:
                    pe.wait_ge(semaphore, n)
                out = take_bank(name, b)
                for k in range(KC):
                    for t in range(T):
                        ins = nc.tensor.transpose(out[:, k * S + t * P:k * S + (t + 1) * P],
                                                  src[:, t, k * P:(k + 1) * P], ident[:])
                ins.then_inc(done, 1)

            def to_features(name, b, w, hi, lo, done, ready):
                for semaphore, n in ready:
                    pe.wait_ge(semaphore, n)
                out = take_bank(name, b)
                for m in range(KC):
                    cols = slice(m * P, (m + 1) * P)
                    ins = product(out[:, m * S:(m + 1) * S],
                                  [(a[:, w, k, cols], z[:, k]) for k in range(KC)
                                   for a, z in ((wh, hi), (wl, hi), (wh, lo))])
                ins.then_inc(done, 1)

            def to_tokens(name, b, w, hi, lo, done, ready):
                for semaphore, n in ready:
                    pe.wait_ge(semaphore, n)
                out = take_bank(name, b)
                for t in range(T):
                    toks = slice(t * P, (t + 1) * P)
                    ins = product(out[:, t * C:(t + 1) * C],
                                  [(z[:, k, toks], a[:, w, k]) for k in range(KC)
                                   for a, z in ((wh, hi), (wl, hi), (wh, lo))])
                ins.then_inc(done, 1)

            def x_T(b):
                transposed("xT", b, zn[:, 0], xT_done, [(zn_ready[0], T * (b + 1))])

            def lin_q(b):
                to_features("lq", b, LQ, xTh, xTl, lq_done, [(xTl_ready, b + 1)])

            def lin_k(b):
                to_tokens("lk", b, LK, xTh, xTl, lk_done, [(xTl_ready, b + 1)])

            def lin_v(b):
                to_tokens("lv", b, LV, xTh, xTl, lv_done, [(xTl_ready, b + 1)])

            def lin_kv(b):
                pe.wait_ge(k1_ready, b + 1)
                pe.wait_ge(v1_ready, b + 1)
                out = take_bank("kv", b)
                for m in range(KC):
                    ins = product(out[:, m * (P + 1):(m + 1) * (P + 1)],
                                  [(k1[:, t, m * P:(m + 1) * P], v1[:, t, m]) for t in range(T)])
                ins.then_inc(kv_done, 1)

            def lin_o(b):
                pe.wait_ge(q1_ready, b + 1)
                pe.wait_ge(kvm_ready, 2 * (b + 1))
                for t in range(T):
                    out = take_bank(f"o{t}", b)
                    for m in range(KC):
                        ins = nc.tensor.matmul(out[:, m * W1:(m + 1) * W1], q1T[:, m, t * P:(t + 1) * P],
                                               kvm[:, m], start=True, stop=True)
                    ins.then_inc(o1_done, 1)

            def o_T(b):
                transposed("oT", b, o1, oT_done, [(o1_ready, T * (b + 1))])

            def lin_out(b):
                to_tokens("x1", b, LO, oTh, oTl, x1_done, [(oTl_ready, b + 1)])

            def y_T(b):
                transposed("yT", b, zn[:, 1], yT_done, [(zn_ready[1], T * (b + 1))])

            def c_T(b):
                transposed("cT", b, cs, cT_done, [(c_loaded, 16 * (b + 1))])

            def cross_q(b):
                to_features("cq", b, CQ, yTh, yTl, cq_done, [(yTl_ready, b + 1)])

            def cross_k(b):
                to_features("ck", b, CK, cTh, cTl, ck_done, [(cTl_ready, b + 1)])

            def cross_v(b):
                to_tokens("cv", b, CV, cTh, cTl, cv_done, [(cTl_ready, b + 1)])

            def scores(b, hp):
                if hp % (HP // KC) == 0:
                    pe.wait_ge(qk_loaded[hp // (HP // KC)], 16 * 6 * (b + 1))
                for t in range(T):
                    wait(pe, s_ready, 2 * H * b + 4 * (hp - 1) + 2 * t + 2)
                    for j in range(2):
                        h = 2 * hp + j
                        ins = nc.tensor.matmul(pS[:, t, j], Q[:, h, t * P:(t + 1) * P], K[:, h], start=True,
                                               stop=True)
                    ins.then_inc(s_done, 1)

            def prob_T(b, hp):
                pe.wait_ge(p_ready, 2 * H * b + 4 * hp + 4)
                for j in range(2):
                    wait(pe, pT_ready[j], HP * b + hp)
                    for k in range(T):
                        for t in range(T):
                            ins = nc.tensor.transpose(pP[:, j, k * S + t * P:k * S + (t + 1) * P],
                                                      sc[:, hp % 4, t, j, k * P:(k + 1) * P], ident[:])
                    ins.then_inc(pT_done, 1)

            def values(b, s, g):
                pe.wait_ge(pT_ready[0], HP * b + 2 * g + 2)
                pe.wait_ge(pT_ready[1], HP * b + 2 * g + 2)
                pe.wait_ge(vx_ready, b + 1)
                wait(pe, oS_ready, G * b + g)
                for k in range(T):
                    for j in range(4):
                        h = 4 * g + j
                        ins = nc.tensor.matmul(pO[32 * j:32 * j + 32, 0:S], vx[:, s, k, h],
                                               PT[:, h % 8, k * S:(k + 1) * S], start=(k == 0), stop=(k == T - 1))
                ins.then_inc(pv_done, 1)

            def outputs_back(b):
                pe.wait_ge(oS_ready, G * (b + 1))
                for t in range(T):
                    out = take_bank(f"n{t}", b)
                    for g in range(G):
                        ins = nc.tensor.transpose(out[:, g * P:(g + 1) * P], oS[:, g, t * P:(t + 1) * P], ident[:])
                    ins.then_inc(nq_done, 1)

            def n_T(b):
                transposed("nT", b, oN, nT_done, [(oN_ready, T * (b + 1))])

            def cross_out(b):
                to_tokens("x2", b, CO, nTh, nTl, x2_done, [(nTl_ready, b + 1)])

            def linear(b):
                x_T(b)
                pe.wait_ge(split_lo, LV + 1)
                lin_k(b)
                lin_q(b)
                lin_v(b)
                lin_kv(b)
                lin_o(b)
                o_T(b)
                pe.wait_ge(split_lo, LO + 1)
                lin_out(b)

            pe.wait_ge(ident_loaded, 16)
            pe.wait_ge(dve_set, 3)
            linear(0)
            c_T(0)
            y_T(0)
            pe.wait_ge(split_lo, CV + 1)
            cross_k(0)
            cross_q(0)
            cross_v(0)
            linear(1)
            pe.wait_ge(split_lo, NW)
            pe.wait_ge(small_loaded, 16 * 7)
            pe.wait_ge(pool_set, 4)
            scores(0, 0)

            def body(b, s):
                A, V, F = b + 2, b + 1, b - 1
                if not isinstance(b, int) or b not in (0, B - 1):
                    occupant[:] = [("o1", b + 1), ("oT", b + 1), ("x1", b + 1)]
                scores(b, 1)
                if has(V):
                    c_T(V)
                if has(F):
                    prob_T(F, 7)
                scores(b, 2)
                if has(F):
                    values(F, 1 - s, 3)
                prob_T(b, 0)
                if has(V):
                    y_T(V)
                if has(A):
                    x_T(A)
                scores(b, 3)
                prob_T(b, 1)
                if has(F):
                    outputs_back(F)
                if has(V):
                    cross_q(V)
                prob_T(b, 2)
                scores(b, 4)
                if has(A):
                    lin_k(A)
                if has(V):
                    cross_k(V)
                if has(A):
                    lin_q(A)
                values(b, s, 0)
                if has(A):
                    lin_v(A)
                scores(b, 5)
                prob_T(b, 3)
                if has(A):
                    lin_kv(A)
                if has(F):
                    n_T(F)
                scores(b, 6)
                values(b, s, 1)
                prob_T(b, 4)
                if has(F):
                    cross_out(F)
                if has(V):
                    cross_v(V)
                if has(A):
                    lin_o(A)
                scores(b, 7)
                prob_T(b, 5)
                if has(A):
                    o_T(A)
                if has(V):
                    scores(V, 0)
                prob_T(b, 6)
                if has(A):
                    lin_out(A)
                values(b, s, 2)

            each_batch(pe, body)
            prob_T(B - 1, 7)
            values(B - 1, 1, 3)
            outputs_back(B - 1)
            n_T(B - 1)
            cross_out(B - 1)


def product(nc, out_ap, terms):
    for i, (lhsT, rhs) in enumerate(terms):
        ins = nc.tensor.matmul(out_ap, lhsT, rhs, start=(i == 0), stop=(i == len(terms) - 1))
    return ins


def build_moe(nc, x2, ident_in, upper_in, ones_in, tri_in, ranks_in, first_rows_in, tokens_in, tiles_in, rW1, rb1,
              rW2, rb2, experts, be1, be2, routed):
    N, C = x2.shape
    E, C = be2.shape
    HID = experts.shape[2]
    RH = rW1.shape[1]
    S = 2 * P
    B = (N - P) // S
    T = S // P
    KC = C // P
    KH = HID // P
    KR = RH // P
    GB = 2
    G = B // GB
    GT = GB * T
    NTOK = B * T
    TS = 2 * P
    FULL = NTOK * P // TS
    NT = 2 * FULL + E
    LAST = E
    REGION = (FULL + 1) * TS
    ROW = routed.shape[1]
    COLS = 1024
    PIECES = experts.shape[0]
    PER_EXPERT = PIECES // E
    PG = PIECES // G
    HALF = 512

    with ExitStack() as ctx:
        wh, wl = (ctx.enter_context(nc.sbuf_tensor(f"m_w{p}", [P, PIECES, COLS], F32R)) for p in "hl")
        b1 = ctx.enter_context(nc.sbuf_tensor("m_b1", [P, E, KH], F32))
        b2 = ctx.enter_context(nc.sbuf_tensor("m_b2", [P, E, C], F32))
        ident = ctx.enter_context(nc.sbuf_tensor("m_ident", [P, P], F32))
        table = ctx.enter_context(nc.sbuf_tensor("m_table", [P, 3, NT], I32))
        build_router(nc, x2, ident, wh, wl, b1, b2, table, ident_in, upper_in, ones_in, tri_in, ranks_in,
                     first_rows_in, tokens_in, tiles_in, rW1, rb1, rW2, rb2, experts, be1, be2,
                     routed, (E, HID, RH, S, B, T, KC, KR, GB, G, GT, NTOK, NT, LAST, TS, FULL, REGION, ROW, COLS,
                              PIECES, PER_EXPERT, PG, HALF))
        build_experts(nc, x2, ident, wh, wl, b1, b2, table, routed,
                      (E, KC, KH, NT, TS, ROW, COLS, PER_EXPERT, HALF))


def build_router(nc, x2, ident, wh, wl, b1, b2, table, ident_in, upper_in, ones_in, tri_in, ranks_in, first_rows_in,
                 tokens_in, tiles_in, rW1, rb1, rW2, rb2, experts, be1, be2, routed, sizes):
    (E, HID, RH, S, B, T, KC, KR, GB, G, GT, NTOK, NT, LAST, TS, FULL, REGION, ROW, COLS, PIECES, PER_EXPERT, PG,
     HALF) = sizes
    N, C = x2.shape
    RING = 4
    with ExitStack() as ctx:
        def sb(name, shape, dt=F32):
            return ctx.enter_context(nc.sbuf_tensor("r_" + name, shape, dt))

        def sem(name):
            return ctx.enter_context(nc.semaphore("r_" + name))

        r1h, r1l = (sb(f"r1{p}", [P, KC, RH], F32R) for p in "hl")
        stage = sb("stage", [P, 2, COLS])
        r2 = sb("r2", [P, KR, E])
        rb1s = sb("rb1", [P, KR])
        rb2s = sb("rb2", [P, E])
        upper = sb("upper", [P, P])
        ones = sb("ones", [P, P])
        tri = sb("tri", [P, E, E])
        ranks = sb("ranks", [P, 2])
        tokens = sb("tokens", [P, NTOK + 1])
        tiles = sb("tiles", [P, NT])
        first_rows = sb("first_rows", [P, E])

        x = sb("x", [P, 2, T, C])
        stats = sb("stats", [P, T, 6])
        mv = sb("mv", [P, T, 2])
        vare = sb("vare", [P, T])
        rstd = sb("rstd", [P, T])
        half_power = sb("half_power", [P, T])
        eps = sb("eps", [P, T])
        rows = sb("rows", [P, RING, GT, ROW])
        pad_row = sb("pad_row", [P, ROW])
        zTh, zTl = (sb(f"zT{p}", [P, 2, KC, S], F32R) for p in "hl")
        rh = sb("rh", [P, 2, KR, S])
        lg = sb("lg", [P, GT, E])
        ex = sb("ex", [P, GT, E])
        prob = sb("prob", [P, GT, E])
        rs = sb("rs", [P, 3, GT])
        above = sb("above", [P, GT, E, E])
        equal = sb("equal", [P, GT, E, E])
        rank = sb("rank", [P, 2, GT, E])
        chosen = sb("chosen", [P, 2, GT, E])
        before = sb("before", [P, 2, GT, E])
        pick = sb("pick", [P, GT, 2, E])
        place = sb("place", [P, GT, 2])
        places = sb("places", [P, RING, GT, 2], I32)
        total = sb("total", [P, 2, E])
        count = sb("count", [P, E])
        bound = sb("bound", [P, E - 1])
        shift = sb("shift", [P, E - 1])
        filled = sb("filled", [P, E], I32)

        after = stage[:].rearrange("p a b -> p (a b)")
        ends = [E * FULL, E * FULL + (E - 1) * NT, E * FULL + 2 * (E - 1) * NT, E * FULL + (2 * E + 1) * NT]
        counted = after[:, 0:ends[0]].rearrange("p (e t) -> p e t", e=E)
        past = after[:, ends[0]:ends[1]].rearrange("p (e t) -> p e t", t=NT)
        moved = after[:, ends[1]:ends[2]].rearrange("p (e t) -> p e t", t=NT)
        entry = after[:, ends[2]:ends[3]].rearrange("p (i t) -> p i t", t=NT)
        tile_row = after[:, ends[3]:ends[3] + NT]

        pZ = ctx.enter_context(nc.psum_tensor("r_pZ", [P, 2, HALF], F32))
        pR = ctx.enter_context(nc.psum_tensor("r_pR", [P, 2, 2, HALF], F32))
        pL = ctx.enter_context(nc.psum_tensor("r_pL", [P, 2, HALF], F32))
        lg_cols, place_cols = slice(0, GT * E), slice(GT * E, 2 * GT * E)

        small_loaded, passed, set_up = sem("small_loaded"), sem("passed"), sem("set_up")
        stage_loaded = [sem(f"stage_loaded{i}") for i in range(2)]
        split_hi, split_lo = sem("split_hi"), sem("split_lo")
        x_loaded = [sem(f"x_loaded{i}") for i in range(2)]
        stats_step, vare_ready, rstd_ready, zn_ready = (sem("stats_step"), sem("vare_ready"), sem("rstd_ready"),
                                                        sem("zn_ready"))
        zT_done, zTh_ready, zTl_ready = sem("zT_done"), sem("zTh_ready"), sem("zTl_ready")
        rh_done, rh_ready, lg_done = sem("rh_done"), sem("rh_ready"), sem("lg_done")
        lg_step, ex_ready, route_step, chosen_ready = (sem("lg_step"), sem("ex_ready"), sem("route_step"),
                                                       sem("chosen_ready"))
        place_done, place_step, places_ready = sem("place_done"), sem("place_step"), sem("places_ready")
        scattered = [sem(f"scattered{i}") for i in range(RING)]
        total_done, table_step, filled_ready, fillers_stored = (sem("total_done"), sem("table_step"),
                                                                sem("filled_ready"), sem("fillers_stored"))
        spare_zeroed, biases_loaded = sem("spare_zeroed"), sem("biases_loaded")
        LG_STEPS, ROUTE_STEPS, PLACE_STEPS = 3, 7, 3
        SMALL = 11

        def each_group(engine, body):
            for g in range(RING):
                body(g, g)
            with engine.Fori(1, G // RING - 1) as i:
                for s in range(RING):
                    body(i * RING + s, s)
            for g in range(G - RING, G + 2):
                body(g, g % RING)

        def has(n, count):
            return not isinstance(n, int) or 0 <= n < count

        def turn(g):
            return g // RING

        block = ctx.enter_context(nc.Block())

        @block.sync
        def _(sp):
            xv = x2[0:B * S].rearrange("(b t p) c -> b p t c", p=P, t=T)

            def load_x(b, s):
                wait_apart(sp, zn_ready, T * (b - 1), passed)
                src = xv[b] if isinstance(b, int) else xv[bass.ds(b, 1)].rearrange("o p t c -> (o p) t c")
                sp.dma_start(x[:, s], src).then_inc(x_loaded[s], 16)

            def load_piece(n, s):
                wait_apart(sp, split_lo, n, passed)
                src = experts[n] if isinstance(n, int) else experts[bass.ds(n, 1)].rearrange("o p c -> (o p) c")
                sp.dma_start(stage[:, s], src).then_inc(stage_loaded[s], 16)

            load_x(0, 0)
            sp.dma_start(stage[:, 1].rearrange("p (k n) -> p k n", k=KC),
                         rW1.rearrange("(k p) n -> p k n", p=P)).then_inc(stage_loaded[1], 16)
            for dst, src in ((ident[:], ident_in), (rb1s[:], rb1), (r2[:], rW2.rearrange("(k p) n -> p k n", p=P)),
                             (rb2s[:], rb2[None, :].broadcast_to([P, E])), (upper[:], upper_in), (ones[:], ones_in),
                             (tri[:], tri_in), (ranks[:], ranks_in), (tokens[:], tokens_in),
                             (tiles[:], tiles_in), (first_rows[:], first_rows_in)):
                sp.dma_start(dst, src).then_inc(small_loaded, 16)
            load_x(1, 1)
            for dst, src in ((b1[:], be1), (b2[:], be2[None, :, :].broadcast_to([P, E, C]))):
                sp.dma_start(dst, src).then_inc(biases_loaded, 16)

            def body(g, s):
                if has(g, G):
                    for q in range(PG):
                        load_piece(g * PG + q, (s * PG + q) % 2)
                    for i in range(GB):
                        if has(g * GB + i + 2, B):
                            load_x(g * GB + i + 2, i)

            each_group(sp, body)
            sp.wait_ge(set_up, 5)
            sp.dma_start(x2[B * S:], pad_row[:, 0:C]).then_inc(spare_zeroed, 16)
            sp.wait_ge(filled_ready, 1)
            with sp.register("filled_row") as row:
                for e in range(E):
                    n = TS + (LAST * TS if e == E - 1 else 0)
                    sp.reg_load(row, filled[0:1, e:e + 1])
                    first = sp.snap(row, min_val=0, max_val=routed.shape[0] - n)
                    sp.dma_start(routed[bass.ds(first, n)].rearrange("(t p) c -> p t c", p=P),
                                 pad_row[:, None, :].broadcast_to([P, n // P, ROW])).then_inc(fillers_stored, 16)
            sp.wait_ge(fillers_stored, 16 * E)
            sp.wait_ge(spare_zeroed, 16)
            sp.wait_ge(biases_loaded, 32)

        @block.scalar
        def _(act):
            act.wait_ge(small_loaded, 16 * SMALL)

            def z_high(b, s):
                act.wait_ge(zT_done, b + 1)
                wait(act, rh_done, 2 * (b - 1))
                nc.scalar.copy(zTh[:, s], pZ[:, s].rearrange("p (k t) -> p k t", k=KC)).then_inc(zTh_ready, 1)

            def gelu(b, s, half):
                wait(act, lg_done, b - 1)
                act.wait_ge(rh_done, 2 * b + half + 1)
                for r in (2 * half, 2 * half + 1):
                    nc.scalar.activation(rh[:, s, r], pR[:, s, r // 2, (r % 2) * S:(r % 2 + 1) * S], ACT.Gelu,
                                         bias=rb1s[:, r:r + 1]).then_inc(rh_ready, 1)

            def split_high(n, slot):
                act.wait_ge(stage_loaded[slot], 16 * (n // 2 + 1 + slot))
                dst = wh[:, n] if isinstance(n, int) else wh[:, bass.ds(n, 1)].rearrange("p o c -> p (o c)")
                nc.scalar.copy(dst, stage[:, slot]).then_inc(split_hi, 1)

            def exps(g):
                act.wait_ge(lg_step, LG_STEPS * (g + 1))
                nc.scalar.activation(ex[:], lg[:], ACT.Exp).then_inc(ex_ready, 1)

            z_high(0, 0)

            def body(g, s):
                if has(g, G):
                    for q in range(PG):
                        split_high(g * PG + q, (s * PG + q) % 2)
                for i in range(GB):
                    b = g * GB + i
                    if has(b + 1, B):
                        z_high(b + 1, 1 - i)
                    if has(g, G):
                        gelu(b, i, 0)
                    if i == 0 and has(g - 1, G):
                        exps(g - 1)
                    if has(g, G):
                        gelu(b, i, 1)
            each_group(act, body)

        @block.vector
        def _(dve):
            nc.vector.memset(rows[:, :, :, C:], 0.0).then_inc(set_up, 1)
            nc.vector.memset(pad_row[:], 0.0).then_inc(set_up, 1)
            def moments(b, s):
                dve.wait_ge(x_loaded[s], 16 * (b // 2 + 1))
                wait(dve, zn_ready, T * b)
                for t in range(T):
                    nc.vector.bn_stats(stats[:, t], x[:, s, t]).then_inc(stats_step, 1)
                wait_apart(dve, stats_step, 2 * T * b + T, passed)
                for t in range(T):
                    nc.vector.bn_aggr(mv[:, t], stats[:, t]).then_inc(stats_step, 1)

            def normalise(b, s, g, gs):
                dve.wait_ge(rstd_ready, b + 1)
                if s == 0:
                    wait(dve, scattered[gs], 16 * 2 * GT * turn(g))
                for t in range(T):
                    nc.vector.tensor_scalar(rows[:, gs, s * T + t, 0:C], x[:, s, t], mv[:, t, 0:1], rstd[:, t:t + 1],
                                            ALU.subtract, ALU.mult).then_inc(zn_ready, 1)

            def z_low(b, s):
                dve.wait_ge(zTh_ready, b + 1)
                nc.vector.tensor_tensor(out=zTl[:, s], in0=pZ[:, s].rearrange("p (k t) -> p k t", k=KC),
                                        in1=zTh[:, s], op=ALU.subtract).then_inc(zTl_ready, 1)

            def split_low(n, slot):
                dve.wait_ge(split_hi, n + 2)
                src, dst = ((wh[:, n], wl[:, n]) if isinstance(n, int) else
                            (w[:, bass.ds(n, 1)].rearrange("p o c -> p (o c)") for w in (wh, wl)))
                nc.vector.tensor_tensor(out=dst, in0=stage[:, slot], in1=src, op=ALU.subtract).then_inc(split_lo, 1)

            def chain(semaphore, base, k, ins):
                ins.then_inc(semaphore, 1)
                dve.wait_ge(semaphore, base + k)

            def wide(a):
                return a[:, :, None].broadcast_to([P, GT, E])

            def logits(g, gs):
                dve.wait_ge(lg_done, GB * (g + 1))
                wait(dve, ex_ready, g)
                base = LG_STEPS * g
                chain(lg_step, base, 1, nc.vector.tensor_tensor(
                    out=lg[:], in0=pL[:, gs % 2, lg_cols].rearrange("p (t e) -> p t e", e=E),
                    in1=rb2s[:, None, :].broadcast_to([P, GT, E]), op=ALU.add))
                chain(lg_step, base, 2, nc.vector.tensor_reduce(out=rs[:, 0], in_=lg[:], axis=AX.X, op=ALU.max))
                nc.vector.tensor_tensor(out=lg[:], in0=lg[:], in1=wide(rs[:, 0]), op=ALU.subtract).then_inc(lg_step, 1)

            def choose(g, gs):
                dve.wait_ge(ex_ready, g + 1)
                wait(dve, place_done, g)
                base = ROUTE_STEPS * g
                r = rank[:, gs % 2]
                chain(route_step, base, 1, nc.vector.tensor_reduce(out=rs[:, 1], in_=ex[:], axis=AX.X, op=ALU.add))
                chain(route_step, base, 2, nc.vector.reciprocal(rs[:, 2], rs[:, 1]))
                chain(route_step, base, 3, nc.vector.tensor_tensor(out=prob[:], in0=ex[:], in1=wide(rs[:, 2]),
                                                                   op=ALU.mult))
                mine = prob[:, :, :, None].broadcast_to([P, GT, E, E])
                other = prob[:, :, None, :].broadcast_to([P, GT, E, E])
                nc.vector.tensor_tensor(out=above[:], in0=other, in1=mine, op=ALU.is_gt).then_inc(route_step, 1)
                chain(route_step, base, 5, nc.vector.tensor_tensor(out=equal[:], in0=other, in1=mine,
                                                                   op=ALU.is_equal))
                chain(route_step, base, 6, nc.vector.tensor_tensor(
                    out=equal[:], in0=equal[:], in1=tri[:, None].broadcast_to([P, GT, E, E]), op=ALU.mult))
                chain(route_step, base, 7, nc.vector.tensor_tensor(out=above[:], in0=above[:], in1=equal[:],
                                                                   op=ALU.add))
                base = CHOSEN_STEPS * g + 1
                chain(chosen_ready, base, 1, nc.vector.tensor_reduce(out=r, in_=above[:], axis=AX.X, op=ALU.add))
                nc.vector.tensor_scalar(chosen[:, gs % 2], r, 1.5, None, ALU.is_lt).then_inc(chosen_ready, 1)
                nc.vector.scalar_tensor_tensor(out=rows[:, gs, :, C:C + E], in0=r, scalar=1.5, in1=prob[:],
                                               op0=ALU.is_lt, op1=ALU.mult).then_inc(chosen_ready, 1)
                numbers = tokens[:, GT * g:GT * (g + 1)] if isinstance(g, int) else tokens[:, bass.ds(g * GT, GT)]
                chain(chosen_ready, base, 4, nc.vector.tensor_copy(rows[:, gs, :, C + E], numbers))
                for t in range(GT):
                    dst = before[:, gs % 2, t + 1] if t + 1 < GT else before[:, 1 - gs % 2, 0]
                    chain(chosen_ready, base, 5 + t, nc.vector.tensor_tensor(
                        out=dst, in0=before[:, gs % 2, t], in1=chosen[:, gs % 2, t], op=ALU.add))

            CHOSEN_STEPS = 4 + GT

            def place_rows(g, gs):
                dve.wait_ge(place_done, g + 1)
                wait(dve, scattered[gs], 16 * 2 * GT * turn(g))
                base = PLACE_STEPS * g
                taken = pL[:, gs % 2, place_cols].rearrange("p (t e) -> p t e", e=E)
                chain(place_step, base, 1, nc.vector.tensor_tensor(
                    out=pick[:], in0=rank[:, gs % 2, :, None, :].broadcast_to([P, GT, 2, E]),
                    in1=ranks[:, None, :, None].broadcast_to([P, GT, 2, E]), op=ALU.is_equal))
                chain(place_step, base, 2, nc.vector.tensor_tensor(
                    out=pick[:], in0=pick[:], in1=taken[:, :, None, :].broadcast_to([P, GT, 2, E]), op=ALU.mult))
                chain(place_step, base, 3, nc.vector.tensor_reduce(out=place[:], in_=pick[:], axis=AX.X, op=ALU.add))
                nc.vector.tensor_copy(places[:, gs], place[:]).then_inc(places_ready, 1)
                dve.wait_ge(places_ready, g + 1)

            moments(0, 0)
            dve.wait_ge(stage_loaded[1], 16)
            router = stage[:, 1].rearrange("p (k n) -> p k n", k=KC)
            nc.vector.tensor_copy(r1h[:], router).then_inc(split_hi, 1)
            dve.wait_ge(split_hi, 1)
            nc.vector.tensor_tensor(out=r1l[:], in0=router, in1=r1h[:], op=ALU.subtract).then_inc(split_lo, 1)
            dve.wait_ge(small_loaded, 16 * SMALL)
            dve.wait_ge(set_up, 4)
            nc.vector.tensor_copy(pad_row[:, C + E:C + E + 1], tokens[:, NTOK:NTOK + 1]).then_inc(set_up, 1)
            nc.vector.tensor_copy(before[:, 0, 0], first_rows[:]).then_inc(chosen_ready, 1)
            dve.wait_ge(chosen_ready, 1)
            normalise(0, 0, 0, 0)
            z_low(0, 0)
            moments(1, 1)
            normalise(1, 1, 0, 0)
            moments(2, 0)

            def body(g, s):
                for i in range(GB):
                    b = g * GB + i
                    if has(b + 2, B):
                        normalise(b + 2, i, g + 1, (s + 1) % RING)
                    if has(b + 1, B):
                        z_low(b + 1, 1 - i)
                    if i == 0 and has(g - 1, G):
                        logits(g - 1, (s - 1) % RING)
                    if has(b + 3, B):
                        moments(b + 3, 1 - i)
                    if i == 0 and has(g - 1, G):
                        choose(g - 1, (s - 1) % RING)
                if has(g - 1, G):
                    place_rows(g - 1, (s - 1) % RING)
                if has(g, G):
                    for q in range(PG):
                        split_low(g * PG + q, (s * PG + q) % 2)

            each_group(dve, body)

            dve.wait_ge(total_done, 1)
            k = [0]

            def step(ins):
                k[0] += 1
                chain(table_step, 0, k[0], ins)

            step(nc.vector.tensor_copy(total[:, 0], pL[:, 0, 0:E]))
            nc.vector.tensor_copy(filled[:], total[:, 0]).then_inc(filled_ready, 1)
            for e in range(E):
                step(nc.vector.tensor_scalar(total[:, 1, e:e + 1], total[:, 0, e:e + 1], float(-e * REGION), None,
                                             ALU.add))
            step(nc.vector.tensor_scalar(tile_row, tiles[:], float(TS), None, ALU.mult))
            step(nc.vector.tensor_tensor(out=counted, in0=total[:, 1, :, None].broadcast_to([P, E, FULL]),
                                         in1=tile_row[:, None, 0:FULL].broadcast_to([P, E, FULL]), op=ALU.is_gt))
            step(nc.vector.tensor_reduce(out=count[:], in_=counted, axis=AX.X, op=ALU.add))
            step(nc.vector.tensor_copy(bound[:, 0:1], count[:, 0:1]))
            for e in range(1, E - 1):
                step(nc.vector.tensor_tensor(out=bound[:, e:e + 1], in0=bound[:, e - 1:e], in1=count[:, e:e + 1],
                                             op=ALU.add))
            step(nc.vector.tensor_scalar(shift[:], count[:, 0:E - 1], float(-TS), float(REGION), ALU.mult, ALU.add))
            step(nc.vector.tensor_tensor(out=past, in0=tiles[:, None, :].broadcast_to([P, E - 1, NT]),
                                         in1=bound[:, :, None].broadcast_to([P, E - 1, NT]), op=ALU.is_ge))
            step(nc.vector.tensor_tensor(out=moved, in0=past,
                                         in1=shift[:, :, None].broadcast_to([P, E - 1, NT]), op=ALU.mult))
            step(nc.vector.tensor_reduce(out=entry[:, 0], in_=past.rearrange("p e t -> p t e"), axis=AX.X,
                                         op=ALU.add))
            step(nc.vector.tensor_reduce(out=entry[:, 2], in_=moved.rearrange("p e t -> p t e"), axis=AX.X,
                                         op=ALU.add))
            step(nc.vector.tensor_scalar(entry[:, 1], entry[:, 0], float(PER_EXPERT), None, ALU.mult))
            step(nc.vector.tensor_tensor(out=entry[:, 2], in0=entry[:, 2], in1=tile_row, op=ALU.add))
            step(nc.vector.tensor_copy(table[:], entry))

        @block.gpsimd
        def _(pool):
            nc.gpsimd.memset(half_power[:], -0.5).then_inc(set_up, 1)
            nc.gpsimd.memset(eps[:], LN_EPS).then_inc(set_up, 1)
            pool.wait_ge(set_up, 4)

            def rsqrt(b):
                pool.wait_ge(stats_step, 2 * T * (b + 1))
                wait(pool, zn_ready, T * b)
                nc.gpsimd.tensor_tensor(out=vare[:], in0=mv[:, :, 1], in1=eps[:], op=ALU.add).then_inc(vare_ready, 1)
                pool.wait_ge(vare_ready, b + 1)
                nc.gpsimd.tensor_tensor(out=rstd[:], in0=vare[:], in1=half_power[:], op=ALU.pow).then_inc(rstd_ready, 1)

            def scatter(g, gs, tiles_of):
                wait_apart(pool, places_ready, g + 1, passed)
                for t in tiles_of:
                    for k in range(2):
                        nc.gpsimd.indirect_dma_start(routed, bass.IndirectOffsetOnAxis(places[:, gs, t, k:k + 1], 0),
                                                     rows[:, gs, t], None).then_inc(scattered[gs], 16)

            rsqrt(0)
            rsqrt(1)
            rsqrt(2)

            def body(g, s):
                for i in range(GB):
                    if has(g - 2, G):
                        scatter(g - 2, (s - 2) % RING, range(i * T, (i + 1) * T))
                    if has(g * GB + i + 3, B):
                        rsqrt(g * GB + i + 3)

            each_group(pool, body)
            for s in range(RING):
                pool.wait_ge(scattered[s], 16 * 2 * GT * (G // RING))

        @block.tensor
        def _(pe):
            def back(b, s, gs):
                pe.wait_ge(zn_ready, T * (b + 1))
                wait(pe, zTl_ready, b - 1)
                for t in range(T):
                    for k in range(KC):
                        ins = nc.tensor.transpose(pZ[:, s, k * S + t * P:k * S + (t + 1) * P],
                                                  rows[:, gs, s * T + t, k * P:(k + 1) * P], ident[:])
                ins.then_inc(zT_done, 1)

            def hidden(b, s, half):
                pe.wait_ge(zTl_ready, b + 1)
                wait(pe, rh_ready, KR * (b - 1))
                for r in (2 * half, 2 * half + 1):
                    cols = slice(r * P, (r + 1) * P)
                    ins = product(nc, pR[:, s, r // 2, (r % 2) * S:(r % 2 + 1) * S],
                                  [(w[:, k, cols], z[:, s, k]) for k in range(KC)
                                   for w, z in ((r1h, zTh), (r1l, zTh), (r1h, zTl))])
                    if r % 2:
                        ins.then_inc(rh_done, 1)

            def logits(b, s, g, gs):
                pe.wait_ge(rh_ready, KR * (b + 1))
                wait(pe, places_ready, g - 1)
                for t in range(T):
                    n = (s * T + t) * E
                    ins = product(nc, pL[:, gs % 2, n:n + E],
                                  [(rh[:, s, k, t * P:(t + 1) * P], r2[:, k]) for k in range(KR)])
                ins.then_inc(lg_done, 1)

            def place(g, gs):
                pe.wait_ge(chosen_ready, 1 + (4 + GT) * (g + 1))
                product(nc, pL[:, gs % 2, place_cols],
                        [(ones[:], before[:, gs % 2].rearrange("p t e -> p (t e)")),
                         (upper[:], chosen[:, gs % 2].rearrange("p t e -> p (t e)"))]).then_inc(place_done, 1)

            pe.wait_ge(small_loaded, 16 * SMALL)
            pe.wait_ge(split_lo, 1)
            back(0, 0, 0)

            def body(g, s):
                for i in range(GB):
                    b = g * GB + i
                    if has(b + 1, B):
                        back(b + 1, 1 - i, (s + i) % RING)
                    if has(g, G):
                        hidden(b, i, 0)
                    if has(b - 1, B):
                        logits(b - 1, 1 - i, *((g, s) if i else (g - 1, (s - 1) % RING)))
                    if i == 1 and has(g - 1, G):
                        place(g - 1, (s - 1) % RING)
                    if has(g, G):
                        hidden(b, i, 1)

            each_group(pe, body)
            pe.wait_ge(places_ready, G)
            nc.tensor.matmul(pL[:, 0, 0:E], ones[:], before[:, G % 2, 0], start=True, stop=True).then_inc(total_done, 1)


def build_experts(nc, x2, ident, wh, wl, b1, b2, table, routed, sizes):
    E, KC, KH, NT, TS, ROW, COLS, PER_EXPERT, HALF = sizes
    C = KC * P
    T = TS // P
    U = KH // 2
    W1P = KC
    PER = COLS // C
    RING = 4
    with ExitStack() as ctx:
        def sb(name, shape, dt=F32):
            return ctx.enter_context(nc.sbuf_tensor("e_" + name, shape, dt))

        def sem(name):
            return ctx.enter_context(nc.semaphore("e_" + name))

        rows = sb("rows", [P, 2, T, ROW])
        gate = sb("gate", [P, RING, T])
        number = sb("number", [P, RING, T], I32)
        bias = sb("bias", [P, 2, KH])
        zTh, zTl = (sb(f"zT{p}", [P, 2, KC, TS], F32R) for p in "hl")
        h = sb("h", [P, 2, 2, TS])
        hh, hl = (sb(f"h{p}", [P, 2, KH, TS], F32R) for p in "hl")
        w1h, w1l = (sb(f"w1{p}", [P, KC, KH * P], F32R) for p in "hl")
        biased = sb("biased", [P, T, C])
        y = sb("y", [P, 2, T, C])

        pZ = ctx.enter_context(nc.psum_tensor("e_pZ", [P, HALF], F32))
        pH = ctx.enter_context(nc.psum_tensor("e_pH", [P, U, HALF], F32))
        pY = ctx.enter_context(nc.psum_tensor("e_pY", [P, T, HALF], F32))

        passed = sem("passed")
        rows_loaded = [sem(f"rows_loaded{i}") for i in range(2)]
        zT_done, zTh_ready, zTl_ready = sem("zT_done"), sem("zTh_ready"), sem("zTl_ready")
        meta_ready, hid_done, h_ready = sem("meta_ready"), sem("hid_done"), sem("h_ready")
        hh_ready, hl_ready = sem("hh_ready"), sem("hl_ready")
        w1h_ready, w1l_ready = sem("w1h_ready"), sem("w1l_ready")
        y_done, biased_ready, y_ready, added = sem("y_done"), sem("biased_ready"), sem("y_ready"), sem("added")
        META = 3

        def each_tile(engine, body):
            for j in range(RING):
                body(j, j)
            with engine.Fori(1, NT // RING - 1) as i:
                for s in range(RING):
                    body(i * RING + s, s)
            for j in range(NT - RING, NT + 2):
                body(j, j % RING)

        def has(j):
            return not isinstance(j, int) or 0 <= j < NT

        def entry(what, j):
            return table[0:1, what, j:j + 1] if isinstance(j, int) else table[0:1, what, bass.ds(j, 1)]

        def of(a, e):
            return a[:, bass.ds(e, 1)].rearrange("p o c -> p (o c)")

        def unit(u):
            return slice(2 * u * P, 2 * (u + 1) * P)

        block = ctx.enter_context(nc.Block())

        @block.sync
        def _(sp):
            with sp.register("row") as row:
                def body(j, s):
                    if not has(j):
                        return
                    wait_apart(sp, zT_done, j - 1, passed)
                    wait_apart(sp, meta_ready, META * (j - 1), passed)
                    sp.reg_load(row, entry(2, j))
                    first = sp.snap(row, min_val=0, max_val=routed.shape[0] - TS)
                    sp.dma_start(rows[:, s % 2], routed[bass.ds(first, TS)].rearrange("(t p) c -> p t c", p=P)
                                 ).then_inc(rows_loaded[s % 2], 16)

                each_tile(sp, body)

        @block.scalar
        def _(act):
            def z_high(j, s):
                act.wait_ge(zT_done, j + 1)
                wait(act, hid_done, U * (j - 1))
                nc.scalar.copy(zTh[:, s % 2], pZ[:].rearrange("p (k t) -> p k t", k=KC)).then_inc(zTh_ready, 1)

            def gelu(j, s, u):
                act.wait_ge(hid_done, U * j + u + 1)
                wait(act, hl_ready, U * j + u - 1)
                for i in range(2):
                    nc.scalar.activation(h[:, u % 2, i], pH[:, u, i * TS:(i + 1) * TS], ACT.Gelu,
                                         bias=bias[:, s % 2, 2 * u + i:2 * u + i + 1]).then_inc(h_ready, 1)

            with act.register("piece") as piece:
                def load_piece(j):
                    act.reg_load(piece, entry(1, j))
                    return wh[:, bass.ds(act.snap(piece, min_val=0, max_val=(E - 1) * PER_EXPERT), W1P)]

                def w1_high(w1, u):
                    nc.scalar.copy(w1h[:, :, unit(u)], w1[:, :, unit(u)]).then_inc(w1h_ready, 1)

                w1 = load_piece(0)
                for u in range(U):
                    w1_high(w1, u)
                z_high(0, 0)

                def body(j, s):
                    if has(j):
                        act.wait_ge(meta_ready, META * (j + 1))
                        w1 = load_piece(j + 1) if has(j + 1) else None
                        for u in range(U):
                            gelu(j, s, u)
                            if has(j + 1):
                                w1_high(w1, u)
                        if has(j + 1):
                            z_high(j + 1, s + 1)

                each_tile(act, body)

        @block.vector
        def _(dve):
            with ExitStack() as regs:
                expert = [regs.enter_context(dve.register(f"expert{i}")) for i in range(RING)]
                piece = [regs.enter_context(dve.register(f"piece{i}")) for i in range(2)]

                def expert_of(s):
                    return dve.snap(expert[s % RING], min_val=0, max_val=E - 1)

                def meta(j, s):
                    dve.wait_ge(rows_loaded[s % 2], 16 * (j // 2 + 1))
                    wait(dve, added, 16 * T * (j - 3))
                    wait(dve, h_ready, KH * (j - 1))
                    dve.reg_load(expert[s % RING], entry(0, j))
                    dve.reg_load(piece[s % 2], entry(1, j))
                    e = expert_of(s)
                    nc.vector.tensor_copy(gate[:, s % RING], rows[:, s % 2, :, bass.ds(e + C, 1)].rearrange(
                        "p t o -> p (t o)")).then_inc(meta_ready, 1)
                    nc.vector.tensor_copy(number[:, s % RING], rows[:, s % 2, :, C + E]).then_inc(meta_ready, 1)
                    nc.vector.tensor_copy(bias[:, s % 2], of(b1, e)).then_inc(meta_ready, 1)

                def z_low(j, s):
                    dve.wait_ge(zTh_ready, j + 1)
                    nc.vector.tensor_tensor(out=zTl[:, s % 2], in0=pZ[:].rearrange("p (k t) -> p k t", k=KC),
                                            in1=zTh[:, s % 2], op=ALU.subtract).then_inc(zTl_ready, 1)

                def w1_low(j, s, u):
                    wait(dve, hid_done, U * (j - 1) + u + 1)
                    low = wl[:, bass.ds(dve.snap(piece[s % 2], min_val=0, max_val=(E - 1) * PER_EXPERT), W1P)]
                    nc.vector.tensor_copy(w1l[:, :, unit(u)], low[:, :, unit(u)]).then_inc(w1l_ready, 1)

                def split_hidden(j, s, units):
                    for u in units:
                        n = U * j + u
                        blocks = slice(2 * u, 2 * u + 2)
                        dve.wait_ge(h_ready, 2 * n + 2)
                        wait(dve, y_done, T * (j - 1))
                        nc.vector.tensor_copy(hh[:, s % 2, blocks], h[:, u % 2]).then_inc(hh_ready, 1)
                        dve.wait_ge(hh_ready, n + 1)
                        nc.vector.tensor_tensor(out=hl[:, s % 2, blocks], in0=h[:, u % 2], in1=hh[:, s % 2, blocks],
                                                op=ALU.subtract).then_inc(hl_ready, 1)

                def output(j, s):
                    e = expert_of(s)
                    wait(dve, y_ready, T * j)
                    for t in range(T):
                        dve.wait_ge(y_done, T * j + t + 1)
                        nc.vector.tensor_tensor(out=biased[:, t], in0=pY[:, t, 0:C], in1=of(b2, e),
                                                op=ALU.add).then_inc(biased_ready, 1)
                    wait(dve, added, 16 * T * (j - 1))
                    for t in range(T):
                        dve.wait_ge(biased_ready, T * j + t + 1)
                        nc.vector.tensor_scalar(y[:, s % 2, t], biased[:, t], gate[:, s % RING, t:t + 1], None,
                                                ALU.mult).then_inc(y_ready, 1)

                meta(0, 0)
                for u in range(U):
                    w1_low(0, 0, u)
                z_low(0, 0)

                def body(j, s):
                    if has(j + 1):
                        meta(j + 1, s + 1)
                    for u in range(U):
                        if has(j):
                            split_hidden(j, s, [u])
                        if has(j + 1):
                            w1_low(j + 1, s + 1, u)
                        if u == 0 and has(j - 2):
                            output(j - 2, s + 2)
                    if has(j + 1):
                        z_low(j + 1, s + 1)

                each_tile(dve, body)

        @block.gpsimd
        def _(pool):
            def body(j, s):
                if not has(j):
                    return
                wait_apart(pool, meta_ready, META * (j + 1), passed)
                for t in range(T):
                    wait_apart(pool, added, 16 * (T * j + t), passed)
                    wait_apart(pool, y_ready, T * j + t + 1, passed)
                    nc.gpsimd.indirect_dma_start(x2, bass.IndirectOffsetOnAxis(number[:, s, t:t + 1], 0),
                                                 y[:, s % 2, t], None, compute_op=ALU.add).then_inc(added, 16)

            each_tile(pool, body)
            pool.wait_ge(added, 16 * T * NT)

        @block.tensor
        def _(pe):
            with ExitStack() as regs:
                piece = [regs.enter_context(pe.register(f"piece{i}")) for i in range(RING)]

                def pieces_of(s):
                    first = pe.snap(piece[s % RING], min_val=0, max_val=(E - 1) * PER_EXPERT)
                    return wh[:, bass.ds(first, PER_EXPERT)], wl[:, bass.ds(first, PER_EXPERT)]

                def back_z(j, s):
                    pe.wait_ge(rows_loaded[s % 2], 16 * (j // 2 + 1))
                    wait(pe, zTl_ready, j)
                    for k in range(KC):
                        for t in range(T):
                            ins = nc.tensor.transpose(pZ[:, k * TS + t * P:k * TS + (t + 1) * P],
                                                      rows[:, s % 2, t, k * P:(k + 1) * P], ident[:])
                    ins.then_inc(zT_done, 1)

                def hidden(j, s):
                    pe.reg_load(piece[s % RING], entry(1, j))
                    pe.wait_ge(zTl_ready, j + 1)
                    for u in range(U):
                        wait(pe, h_ready, KH * (j - 1) + 2 * u + 2)
                        pe.wait_ge(w1h_ready, U * j + u + 1)
                        pe.wait_ge(w1l_ready, U * j + u + 1)
                        for i in range(2):
                            cols = slice((2 * u + i) * P, (2 * u + i + 1) * P)
                            ins = product(nc, pH[:, u, i * TS:(i + 1) * TS],
                                          [(w[:, k, cols], z[:, s % 2, k]) for k in range(KC)
                                           for z, w in ((zTh, w1h), (zTl, w1h), (zTh, w1l))])
                        ins.then_inc(hid_done, 1)

                def output(j, s):
                    pe.wait_ge(hl_ready, U * (j + 1))
                    wait(pe, biased_ready, T * j)
                    high, low = pieces_of(s)
                    for t in range(T):
                        product(nc, pY[:, t, 0:C],
                                [(a[:, s % 2, k, t * P:(t + 1) * P],
                                  w[:, W1P + k // PER, k % PER * C:(k % PER + 1) * C]) for k in range(KH)
                                 for a, w in ((hh, high), (hl, high), (hh, low))]).then_inc(y_done, 1)

                back_z(0, 0)

                def body(j, s):
                    if has(j):
                        hidden(j, s)
                    if has(j + 1):
                        back_z(j + 1, s + 1)
                    if has(j - 1):
                        output(j - 1, s + 3)

                each_tile(pe, body)


def build_layer(nc, a, routed_shape, out):
    B, S, C = a["x"].shape
    after_attention = out[0:B * S].rearrange("(b s) c -> b s c", s=S)
    qk = nc.dram_tensor("qk_scratch", (B, 4, C, S), F32, kind="Internal").ap()
    routed = nc.dram_tensor("routed_scratch", routed_shape, F32, kind="Internal").ap()
    build_attention(nc, a["x"], a["ctx"], a["mask"], a["ident"], a["blocks"], a["heads"], a["wqkvT"], a["woutT"],
                    a["b_out"], a["wqT"], a["bq"], a["wkT"], a["bk"], a["wvT"], a["bv"], a["woT"], a["bo"], qk,
                    after_attention)
    build_moe(nc, out, a["ident"], a["upper"], a["ones"], a["tri"], a["ranks"], a["first_rows"], a["tokens"],
              a["tiles"], a["rW1"], a["rb1"], a["rW2"], a["rb2"], a["experts"], a["be1"],
              a["be2"], routed)


def routing_constants(np, N, C, E):
    ntok = N // P
    rows = np.arange(P, dtype=np.float32)[:, None]
    tile = 2 * P
    full = N // tile
    region = (full + 1) * tile
    first = np.zeros((P, E), np.float32)
    first[0] = region * np.arange(E)
    arrays = {
        "ident": np.eye(P, dtype=np.float32), "upper": np.triu(np.ones((P, P), np.float32), 1),
        "ones": np.ones((P, P), np.float32),
        "tri": np.broadcast_to(np.tril(np.ones((E, E), np.float32), -1), (P, E, E)),
        "ranks": np.broadcast_to(np.arange(2, dtype=np.float32), (P, 2)), "first_rows": first,
        "tokens": rows + P * np.arange(ntok + 1, dtype=np.float32),
        "tiles": np.broadcast_to(np.arange(2 * full + E, dtype=np.float32), (P, 2 * full + E)),
    }
    line = 8
    width = -(-(C + E + 1) // line) * line
    return arrays, (E * region + E * tile, width)


def expert_arrays(np, f):
    E, C, HID = f["L0_ffn_We1"].shape
    w1 = f["L0_ffn_We1"].reshape(E, C // P, P, HID)
    w2 = f["L0_ffn_We2"].reshape(E, C // P, -1, P, C).transpose(0, 1, 3, 2, 4).reshape(E, C // P, P, HID)
    return {"rW1": f["L0_ffn_rW1"], "rb1": f["L0_ffn_rb1"].reshape(-1, P).T, "rW2": f["L0_ffn_rW2"],
            "rb2": f["L0_ffn_rb2"], "experts": np.concatenate([w1, w2], axis=1).reshape(-1, P, HID),
            "be1": f["L0_ffn_be1"].reshape(E, -1, P).transpose(2, 0, 1), "be2": f["L0_ffn_be2"]}


def kernel(**inputs):
    import numpy as np
    import concourse.bacc as bacc
    from concourse.bass_utils import run_bass_kernel_spmd

    f = {k: np.asarray(v) for k, v in inputs.items()}
    B, S, C = f["x"].shape
    D = C // HEADS
    block = np.kron(np.eye(P // D), np.full((D, D), D ** -0.5)).astype(np.float32)
    constants, routed_shape = routing_constants(np, B * S, C, f["L0_ffn_be1"].shape[0])
    arrays = {
        "x": f["x"], "ctx": f["ctx_1024"], "mask": f["mask_BxSxS2_ff0"],
        "blocks": block, "heads": np.ascontiguousarray(block[:, ::D]),
        "wqkvT": f["L0_attn_w_qkv"].T, "woutT": f["L0_attn_w_out"].T, "b_out": f["L0_attn_b_out"],
        "wqT": f["L0_xattn_Wq"].T, "bq": f["L0_xattn_bq"].reshape(-1, P).T,
        "wkT": f["L0_xattn_Wk"].T, "bk": f["L0_xattn_bk"].reshape(-1, P).T,
        "wvT": f["L0_xattn_Wv"].T, "bv": f["L0_xattn_bv"],
        "woT": f["L0_xattn_Wo"].T, "bo": f["L0_xattn_bo"],
    } | constants | expert_arrays(np, f)
    arrays = {k: np.ascontiguousarray(v) for k, v in arrays.items()}
    nc = bacc.Bacc("TRN2", target_bir_lowering=False, num_devices=1)
    a = {k: nc.dram_tensor(k, v.shape, mybir.dt.from_np(v.dtype), kind="ExternalInput").ap()
         for k, v in arrays.items()}
    out = nc.dram_tensor("out", (B * S + P, C), F32, kind="ExternalOutput").ap()
    build_layer(nc, a, routed_shape, out)
    r = run_bass_kernel_spmd(nc, [arrays], core_ids=[0])
    return r.results[0]["out"][:B * S].reshape(B, S, C)
```
